# Optimizing a Trainium2 kernel written in Bass

```python
import numpy as np
import jax
import jax.numpy as jnp

def _softmax(x, axis=-1):
    return jax.nn.softmax(x, axis=axis)

def _gelu(x):
    return jax.nn.gelu(x, approximate=True)

def _silu(x):
    return jax.nn.silu(x)

def _sigmoid(x):
    return jax.nn.sigmoid(x)

def _layernorm(x, axis=-1, eps=1e-05):
    m = jnp.mean(x, axis=axis, keepdims=True)
    v = jnp.var(x, axis=axis, keepdims=True)
    return (x - m) / jnp.sqrt(v + eps)

def _scatter_add(tgt, idx, src, axis=0):
    return tgt.at[idx].add(src)

def _segment_sum(src, seg, n):
    return jax.ops.segment_sum(src, seg, n)
kernel_name = 'mk_lm_tower_d1_tok_ids768_r4_fbc7b5'

def setup_inputs(seed: int=0):
    np.random.seed(seed)
    _w = jnp.asarray

    def _rec_inputs():
        import jax
        import jax.numpy as jnp
        _rk = jax.random.key(seed)
        x = jax.random.randint(jax.random.fold_in(_rk, 1), (64, 128), 0, 30522, jnp.int32)
        mask_BS_i0_1 = jnp.where(jnp.ones((64, 128), dtype=bool), 0, 1).astype(jnp.int32)
        return (x, mask_BS_i0_1)
    x, mask_BS_i0_1 = _rec_inputs()

    def _L0_tok_setup():
        import jax, jax.numpy as jnp
        import numpy as np
        V, H, NH, FF, L = (30522, 192, 12, 768, 2)
        B, S = (64, 128)
        EPS = 1e-12

        def _ln(x, g, b):
            m = x.mean(-1, keepdims=True)
            v = jnp.var(x, axis=-1, keepdims=True)
            return (x - m) / jnp.sqrt(v + EPS) * g + b

        def _forward(input_ids, token_type_ids, word_emb, pos_emb3, type_emb, emb_ln_g, emb_ln_b, Wq, bq, Wk, bk, Wv, bv, Wo, bo, ln1_g, ln1_b, W1, b1, W2, b2, ln2_g, ln2_b, Wg, bg, pos_emb2, type_emb2, norm_g, norm_b):
            b, s = input_ids.shape
            prev = jnp.pad(input_ids, ((0, 0), (1, 0)))[:, :-1]
            nxt = jnp.pad(input_ids, ((0, 0), (0, 1)))[:, 1:]
            tri = jnp.stack([prev, input_ids, nxt], -1)
            tri = jnp.concatenate([tri, jnp.zeros((b, 1, 3), tri.dtype)], 1)
            tri = tri.reshape(b * (s + 1), 3)
            mask = (tri > 0).astype(jnp.float32).at[:, 1].set(1.0)
            bias = (1.0 - mask)[:, None, None, :] * -10000.0
            x = word_emb[tri] + pos_emb3[None] + type_emb[0][None, None]
            x = _ln(x, emb_ln_g, emb_ln_b)
            dh = H // NH
            scale = float(1.0 / np.sqrt(dh))
            for i in range(L):
                q = (x @ Wq[i] + bq[i]).reshape(-1, 3, NH, dh)
                k = (x @ Wk[i] + bk[i]).reshape(-1, 3, NH, dh)
                v = (x @ Wv[i] + bv[i]).reshape(-1, 3, NH, dh)
                scores = jnp.einsum('nqhd,nkhd->nhqk', q, k) * scale + bias
                a = jax.nn.softmax(scores, -1)
                c = jnp.einsum('nhqk,nkhd->nqhd', a, v).reshape(-1, 3, H)
                x = _ln(x + c @ Wo[i] + bo[i], ln1_g[i], ln1_b[i])
                f = jax.nn.gelu(x @ W1[i] + b1[i], approximate=False)
                x = _ln(x + f @ W2[i] + b2[i], ln2_g[i], ln2_b[i])
            center_ok = (tri[:, 1] > 0).astype(x.dtype)
            x = x * center_ok[:, None, None]
            x = x * jax.nn.sigmoid(x @ Wg + bg) * mask[..., None]
            flat = x[:, 1]
            flat = flat.at[:-1].add(x[1:, 0]).at[1:].add(x[:-1, 2])
            hs = flat.reshape(b, s + 1, H)[:, :s]
            aux = pos_emb2[None, :s] + type_emb2[token_type_ids]
            return _ln(hs + aux, norm_g, norm_b)
        key = jax.random.key(seed)
        ks = jax.random.split(key, 16)
        p = lambda k, shape: jax.random.normal(k, shape, jnp.float32) * 0.02
        return {'input_ids': jax.random.randint(ks[0], (B, S), 1, V).astype(jnp.int32), 'token_type_ids': jnp.zeros((B, S), jnp.int32), 'word_emb': p(ks[1], (V, H)), 'pos_emb3': p(ks[2], (3, H)), 'type_emb': p(ks[3], (2, H)), 'emb_ln_g': jnp.ones((H,)), 'emb_ln_b': jnp.zeros((H,)), 'Wq': p(ks[4], (L, H, H)), 'bq': jnp.zeros((L, H)), 'Wk': p(ks[5], (L, H, H)), 'bk': jnp.zeros((L, H)), 'Wv': p(ks[6], (L, H, H)), 'bv': jnp.zeros((L, H)), 'Wo': p(ks[7], (L, H, H)), 'bo': jnp.zeros((L, H)), 'ln1_g': jnp.ones((L, H)), 'ln1_b': jnp.zeros((L, H)), 'W1': p(ks[8], (L, H, FF)), 'b1': jnp.zeros((L, FF)), 'W2': p(ks[9], (L, FF, H)), 'b2': jnp.zeros((L, H)), 'ln2_g': jnp.ones((L, H)), 'ln2_b': jnp.zeros((L, H)), 'Wg': p(ks[10], (H, H)), 'bg': jnp.zeros((H,)), 'pos_emb2': p(ks[11], (S, H)), 'type_emb2': p(ks[12], (2, H)), 'norm_g': jnp.ones((H,)), 'norm_b': jnp.zeros((H,))}
    _L0_tok_all = _L0_tok_setup()
    _L0_tok_in = {k: v for k, v in _L0_tok_all.items() if k in ('word_emb', 'pos_emb3', 'type_emb', 'emb_ln_g', 'emb_ln_b', 'Wq', 'bq', 'Wk', 'bk', 'Wv', 'bv', 'Wo', 'bo', 'ln1_g', 'ln1_b', 'W1', 'b1', 'W2', 'b2', 'ln2_g', 'ln2_b', 'Wg', 'bg', 'pos_emb2', 'type_emb2', 'norm_g', 'norm_b')}
    del _L0_tok_all

    def _L0_attn_setup():
        import jax, jax.numpy as jnp
        import numpy as np
        HIDDEN = 192
        NUM_HEADS = 12
        HEAD_DIM = 64

        def _xavier(key, shape):
            fan_in, fan_out = (shape[1], shape[0])
            limit = float(np.sqrt(6.0 / (fan_in + fan_out)))
            return jax.random.uniform(key, shape, jnp.float32, -limit, limit)
        key = jax.random.key(seed)
        k1, k2, k3 = jax.random.split(key, 3)
        B, N = (4, 512)
        x = jax.random.normal(k1, (B, N, HIDDEN), dtype=jnp.float32)
        qkv_w = _xavier(k2, (3 * NUM_HEADS * HEAD_DIM, HIDDEN))
        qkv_b = jnp.zeros((3 * NUM_HEADS * HEAD_DIM,), jnp.float32)
        proj_w = _xavier(k3, (HIDDEN, NUM_HEADS * HEAD_DIM))
        proj_b = jnp.zeros((HIDDEN,), jnp.float32)
        return {'x': x, 'qkv_w': qkv_w, 'qkv_b': qkv_b, 'proj_w': proj_w, 'proj_b': proj_b}
    _L0_attn_all = _L0_attn_setup()
    _L0_attn_in = {k: v for k, v in _L0_attn_all.items() if k in ('qkv_w', 'qkv_b', 'proj_w', 'proj_b')}
    del _L0_attn_all

    def _L0_ffn_setup():
        import jax, jax.numpy as jnp
        import numpy as np
        DIM = 192
        HEADS = 12
        HD = DIM // HEADS
        MLP = 768
        RHD = 128
        RANK = 64
        BS = 2
        RESERVE = 1
        EPS = 1e-05

        def _ln(x, g, b):
            m = jnp.mean(x, axis=-1, keepdims=True)
            v = jnp.var(x, axis=-1, keepdims=True)
            return (x - m) / jnp.sqrt(v + EPS) * g + b

        def _gelu(t):
            return jax.nn.gelu(t, approximate=False)

        def _forward(x, wq, bq, wk, bk, wv, bv, wo, bo, ln1_g, ln1_b, ln2_g, ln2_b, fc1_w, fc1_b, fc2_w, fc2_b, r_ln_g, r_ln_b, r_in_w, r_in_b, r_o1_w, r_o1_b, r_o2_w, r_o2_b, r_o3_w, r_o3_b, lra_down, lra_up):
            B, N, _ = x.shape
            e = _gelu(_ln(x, r_ln_g, r_ln_b) @ r_in_w.T + r_in_b)
            g = jnp.mean(e[:, RESERVE:, :], axis=1, keepdims=True)
            f = jnp.concatenate([e, jnp.broadcast_to(g, e.shape)], axis=-1)
            h1 = _gelu(f @ r_o1_w.T + r_o1_b)
            h2 = _gelu(h1 @ r_o2_w.T + r_o2_b)
            logits = (h2 @ r_o3_w.T + r_o3_b).reshape(B, N, BS, 2)
            hard = jax.nn.one_hot(jnp.argmax(logits, axis=-1), 2, dtype=x.dtype)
            keep = jnp.broadcast_to(jnp.array([0.0, 1.0], dtype=x.dtype), hard[:, :RESERVE].shape)
            hard = hard.at[:, :RESERVE].set(keep)
            hard = jax.lax.stop_gradient(hard)
            bits = hard[..., 1]
            indices = (bits * jnp.array([2.0, 1.0], dtype=x.dtype)).sum(-1).astype(jnp.int32)
            indices = jax.lax.stop_gradient(indices)
            xa = _ln(x, ln1_g, ln1_b)
            q = (xa @ wq.T + bq).reshape(B, N, HEADS, HD).transpose(0, 2, 1, 3)
            k = (xa @ wk.T + bk).reshape(B, N, HEADS, HD).transpose(0, 2, 1, 3)
            v = (xa @ wv.T + bv).reshape(B, N, HEADS, HD).transpose(0, 2, 1, 3)
            s = jax.nn.softmax(jnp.einsum('bhqd,bhkd->bhqk', q, k) / np.float32(np.sqrt(HD)), axis=-1)
            o = jnp.einsum('bhqk,bhkd->bhqd', s, v).transpose(0, 2, 1, 3).reshape(B, N, DIM)
            o = o @ wo.T + bo
            h = x + bits[:, :, 0:1] * o
            xf = _ln(h, ln2_g, ln2_b)
            ff = _gelu(xf @ fc1_w.T + fc1_b) @ fc2_w.T + fc2_b
            out = h + bits[:, :, 1:2] * ff
            down = jnp.einsum('bnd,krd->bknr', out, lra_down)
            up = jnp.einsum('bknr,kdr->bknd', down, lra_up)
            sel = jax.nn.one_hot(indices, 3, dtype=x.dtype)
            out = out + jnp.einsum('bknd,bnk->bnd', up, sel)
            return out
        key = jax.random.key(seed)
        ks = iter(jax.random.split(key, 40))

        def w(shape, std=0.02):
            return (jax.random.normal(next(ks), shape) * std).astype(jnp.float32)
        B, N = (128, 197)
        inp = {'x': jax.random.normal(next(ks), (B, N, DIM), dtype=jnp.float32)}
        inp.update(wq=w((DIM, DIM)), bq=jnp.zeros((DIM,), jnp.float32), wk=w((DIM, DIM)), bk=jnp.zeros((DIM,), jnp.float32), wv=w((DIM, DIM)), bv=jnp.zeros((DIM,), jnp.float32), wo=w((DIM, DIM)), bo=jnp.zeros((DIM,), jnp.float32), ln1_g=jnp.ones((DIM,), jnp.float32), ln1_b=jnp.zeros((DIM,), jnp.float32), ln2_g=jnp.ones((DIM,), jnp.float32), ln2_b=jnp.zeros((DIM,), jnp.float32), fc1_w=w((MLP, DIM)), fc1_b=jnp.zeros((MLP,), jnp.float32), fc2_w=w((DIM, MLP)), fc2_b=jnp.zeros((DIM,), jnp.float32), r_ln_g=jnp.ones((DIM,), jnp.float32), r_ln_b=jnp.zeros((DIM,), jnp.float32), r_in_w=w((RHD, DIM)), r_in_b=jnp.zeros((RHD,), jnp.float32), r_o1_w=w((RHD, 2 * RHD)), r_o1_b=jnp.zeros((RHD,), jnp.float32), r_o2_w=w((RHD // 2, RHD)), r_o2_b=jnp.zeros((RHD // 2,), jnp.float32), r_o3_w=w((2 * BS, RHD // 2), 0.01), r_o3_b=jnp.array([0.0, 5.0, 0.0, 5.0], dtype=jnp.float32), lra_down=w((3, RANK, DIM), 0.01), lra_up=w((3, DIM, RANK), 0.01))
        return inp
    _L0_ffn_all = _L0_ffn_setup()
    _L0_ffn_in = {k: v for k, v in _L0_ffn_all.items() if k in ('wq', 'bq', 'wk', 'bk', 'wv', 'bv', 'wo', 'bo', 'ln1_g', 'ln1_b', 'ln2_g', 'ln2_b', 'fc1_w', 'fc1_b', 'fc2_w', 'fc2_b', 'r_ln_g', 'r_ln_b', 'r_in_w', 'r_in_b', 'r_o1_w', 'r_o1_b', 'r_o2_w', 'r_o2_b', 'r_o3_w', 'r_o3_b', 'lra_down', 'lra_up')}
    del _L0_ffn_all
    return {'x': x, 'mask_BS_i0_1': mask_BS_i0_1, 'L0_tok_word_emb': _L0_tok_in['word_emb'], 'L0_tok_pos_emb3': _L0_tok_in['pos_emb3'], 'L0_tok_type_emb': _L0_tok_in['type_emb'], 'L0_tok_emb_ln_g': _L0_tok_in['emb_ln_g'], 'L0_tok_emb_ln_b': _L0_tok_in['emb_ln_b'], 'L0_tok_Wq': _L0_tok_in['Wq'], 'L0_tok_bq': _L0_tok_in['bq'], 'L0_tok_Wk': _L0_tok_in['Wk'], 'L0_tok_bk': _L0_tok_in['bk'], 'L0_tok_Wv': _L0_tok_in['Wv'], 'L0_tok_bv': _L0_tok_in['bv'], 'L0_tok_Wo': _L0_tok_in['Wo'], 'L0_tok_bo': _L0_tok_in['bo'], 'L0_tok_ln1_g': _L0_tok_in['ln1_g'], 'L0_tok_ln1_b': _L0_tok_in['ln1_b'], 'L0_tok_W1': _L0_tok_in['W1'], 'L0_tok_b1': _L0_tok_in['b1'], 'L0_tok_W2': _L0_tok_in['W2'], 'L0_tok_b2': _L0_tok_in['b2'], 'L0_tok_ln2_g': _L0_tok_in['ln2_g'], 'L0_tok_ln2_b': _L0_tok_in['ln2_b'], 'L0_tok_Wg': _L0_tok_in['Wg'], 'L0_tok_bg': _L0_tok_in['bg'], 'L0_tok_pos_emb2': _L0_tok_in['pos_emb2'], 'L0_tok_type_emb2': _L0_tok_in['type_emb2'], 'L0_tok_norm_g': _L0_tok_in['norm_g'], 'L0_tok_norm_b': _L0_tok_in['norm_b'], 'L0_attn_qkv_w': _L0_attn_in['qkv_w'], 'L0_attn_qkv_b': _L0_attn_in['qkv_b'], 'L0_attn_proj_w': _L0_attn_in['proj_w'], 'L0_attn_proj_b': _L0_attn_in['proj_b'], 'L0_ffn_wq': _L0_ffn_in['wq'], 'L0_ffn_bq': _L0_ffn_in['bq'], 'L0_ffn_wk': _L0_ffn_in['wk'], 'L0_ffn_bk': _L0_ffn_in['bk'], 'L0_ffn_wv': _L0_ffn_in['wv'], 'L0_ffn_bv': _L0_ffn_in['bv'], 'L0_ffn_wo': _L0_ffn_in['wo'], 'L0_ffn_bo': _L0_ffn_in['bo'], 'L0_ffn_ln1_g': _L0_ffn_in['ln1_g'], 'L0_ffn_ln1_b': _L0_ffn_in['ln1_b'], 'L0_ffn_ln2_g': _L0_ffn_in['ln2_g'], 'L0_ffn_ln2_b': _L0_ffn_in['ln2_b'], 'L0_ffn_fc1_w': _L0_ffn_in['fc1_w'], 'L0_ffn_fc1_b': _L0_ffn_in['fc1_b'], 'L0_ffn_fc2_w': _L0_ffn_in['fc2_w'], 'L0_ffn_fc2_b': _L0_ffn_in['fc2_b'], 'L0_ffn_r_ln_g': _L0_ffn_in['r_ln_g'], 'L0_ffn_r_ln_b': _L0_ffn_in['r_ln_b'], 'L0_ffn_r_in_w': _L0_ffn_in['r_in_w'], 'L0_ffn_r_in_b': _L0_ffn_in['r_in_b'], 'L0_ffn_r_o1_w': _L0_ffn_in['r_o1_w'], 'L0_ffn_r_o1_b': _L0_ffn_in['r_o1_b'], 'L0_ffn_r_o2_w': _L0_ffn_in['r_o2_w'], 'L0_ffn_r_o2_b': _L0_ffn_in['r_o2_b'], 'L0_ffn_r_o3_w': _L0_ffn_in['r_o3_w'], 'L0_ffn_r_o3_b': _L0_ffn_in['r_o3_b'], 'L0_ffn_lra_down': _L0_ffn_in['lra_down'], 'L0_ffn_lra_up': _L0_ffn_in['lra_up']}

def reference(x, mask_BS_i0_1, L0_tok_word_emb, L0_tok_pos_emb3, L0_tok_type_emb, L0_tok_emb_ln_g, L0_tok_emb_ln_b, L0_tok_Wq, L0_tok_bq, L0_tok_Wk, L0_tok_bk, L0_tok_Wv, L0_tok_bv, L0_tok_Wo, L0_tok_bo, L0_tok_ln1_g, L0_tok_ln1_b, L0_tok_W1, L0_tok_b1, L0_tok_W2, L0_tok_b2, L0_tok_ln2_g, L0_tok_ln2_b, L0_tok_Wg, L0_tok_bg, L0_tok_pos_emb2, L0_tok_type_emb2, L0_tok_norm_g, L0_tok_norm_b, L0_attn_qkv_w, L0_attn_qkv_b, L0_attn_proj_w, L0_attn_proj_b, L0_ffn_wq, L0_ffn_bq, L0_ffn_wk, L0_ffn_bk, L0_ffn_wv, L0_ffn_bv, L0_ffn_wo, L0_ffn_bo, L0_ffn_ln1_g, L0_ffn_ln1_b, L0_ffn_ln2_g, L0_ffn_ln2_b, L0_ffn_fc1_w, L0_ffn_fc1_b, L0_ffn_fc2_w, L0_ffn_fc2_b, L0_ffn_r_ln_g, L0_ffn_r_ln_b, L0_ffn_r_in_w, L0_ffn_r_in_b, L0_ffn_r_o1_w, L0_ffn_r_o1_b, L0_ffn_r_o2_w, L0_ffn_r_o2_b, L0_ffn_r_o3_w, L0_ffn_r_o3_b, L0_ffn_lra_down, L0_ffn_lra_up):
    import jax
    import jax.numpy as jnp

    def _L0_tok_ref(input_ids, token_type_ids, word_emb, pos_emb3, type_emb, emb_ln_g, emb_ln_b, Wq, bq, Wk, bk, Wv, bv, Wo, bo, ln1_g, ln1_b, W1, b1, W2, b2, ln2_g, ln2_b, Wg, bg, pos_emb2, type_emb2, norm_g, norm_b):
        import jax, jax.numpy as jnp
        import numpy as np
        V, H, NH, FF, L = (30522, 192, 12, 768, 2)
        B, S = (64, 128)
        EPS = 1e-12

        def _ln(x, g, b):
            m = x.mean(-1, keepdims=True)
            v = jnp.var(x, axis=-1, keepdims=True)
            return (x - m) / jnp.sqrt(v + EPS) * g + b

        def _forward(input_ids, token_type_ids, word_emb, pos_emb3, type_emb, emb_ln_g, emb_ln_b, Wq, bq, Wk, bk, Wv, bv, Wo, bo, ln1_g, ln1_b, W1, b1, W2, b2, ln2_g, ln2_b, Wg, bg, pos_emb2, type_emb2, norm_g, norm_b):
            b, s = input_ids.shape
            prev = jnp.pad(input_ids, ((0, 0), (1, 0)))[:, :-1]
            nxt = jnp.pad(input_ids, ((0, 0), (0, 1)))[:, 1:]
            tri = jnp.stack([prev, input_ids, nxt], -1)
            tri = jnp.concatenate([tri, jnp.zeros((b, 1, 3), tri.dtype)], 1)
            tri = tri.reshape(b * (s + 1), 3)
            mask = (tri > 0).astype(jnp.float32).at[:, 1].set(1.0)
            bias = (1.0 - mask)[:, None, None, :] * -10000.0
            x = word_emb[tri] + pos_emb3[None] + type_emb[0][None, None]
            x = _ln(x, emb_ln_g, emb_ln_b)
            dh = H // NH
            scale = float(1.0 / np.sqrt(dh))
            for i in range(L):
                q = (x @ Wq[i] + bq[i]).reshape(-1, 3, NH, dh)
                k = (x @ Wk[i] + bk[i]).reshape(-1, 3, NH, dh)
                v = (x @ Wv[i] + bv[i]).reshape(-1, 3, NH, dh)
                scores = jnp.einsum('nqhd,nkhd->nhqk', q, k) * scale + bias
                a = jax.nn.softmax(scores, -1)
                c = jnp.einsum('nhqk,nkhd->nqhd', a, v).reshape(-1, 3, H)
                x = _ln(x + c @ Wo[i] + bo[i], ln1_g[i], ln1_b[i])
                f = jax.nn.gelu(x @ W1[i] + b1[i], approximate=False)
                x = _ln(x + f @ W2[i] + b2[i], ln2_g[i], ln2_b[i])
            center_ok = (tri[:, 1] > 0).astype(x.dtype)
            x = x * center_ok[:, None, None]
            x = x * jax.nn.sigmoid(x @ Wg + bg) * mask[..., None]
            flat = x[:, 1]
            flat = flat.at[:-1].add(x[1:, 0]).at[1:].add(x[:-1, 2])
            hs = flat.reshape(b, s + 1, H)[:, :s]
            aux = pos_emb2[None, :s] + type_emb2[token_type_ids]
            return _ln(hs + aux, norm_g, norm_b)
        return _forward(input_ids, token_type_ids, word_emb, pos_emb3, type_emb, emb_ln_g, emb_ln_b, Wq, bq, Wk, bk, Wv, bv, Wo, bo, ln1_g, ln1_b, W1, b1, W2, b2, ln2_g, ln2_b, Wg, bg, pos_emb2, type_emb2, norm_g, norm_b)

    def _L0_attn_ref(x, qkv_w, qkv_b, proj_w, proj_b):
        import jax, jax.numpy as jnp
        import numpy as np
        HIDDEN = 192
        NUM_HEADS = 12
        HEAD_DIM = 64

        def _xavier(key, shape):
            fan_in, fan_out = (shape[1], shape[0])
            limit = float(np.sqrt(6.0 / (fan_in + fan_out)))
            return jax.random.uniform(key, shape, jnp.float32, -limit, limit)
        B, N, _ = x.shape
        nh, H = (NUM_HEADS, HEAD_DIM)
        qkv = jnp.einsum('bnd,od->bno', x, qkv_w) + qkv_b
        q, k, v = jnp.split(qkv, 3, axis=-1)

        def heads(t):
            return t.reshape(B, N, nh, H).transpose(0, 2, 1, 3)
        q, k, v = (heads(q), heads(k), heads(v))
        scores = jnp.einsum('bhnd,bhmd->bhnm', q, k) / jnp.sqrt(jnp.float32(H))
        attn = jax.nn.softmax(scores, axis=-1)
        out = jnp.einsum('bhnm,bhmd->bhnd', attn, v)
        out = out.transpose(0, 2, 1, 3).reshape(B, N, nh * H)
        out = jnp.einsum('bnk,ok->bno', out, proj_w) + proj_b
        return out

    def _L0_ffn_ref(x, wq, bq, wk, bk, wv, bv, wo, bo, ln1_g, ln1_b, ln2_g, ln2_b, fc1_w, fc1_b, fc2_w, fc2_b, r_ln_g, r_ln_b, r_in_w, r_in_b, r_o1_w, r_o1_b, r_o2_w, r_o2_b, r_o3_w, r_o3_b, lra_down, lra_up):
        import jax, jax.numpy as jnp
        import numpy as np
        DIM = 192
        HEADS = 12
        HD = DIM // HEADS
        MLP = 768
        RHD = 128
        RANK = 64
        BS = 2
        RESERVE = 1
        EPS = 1e-05

        def _ln(x, g, b):
            m = jnp.mean(x, axis=-1, keepdims=True)
            v = jnp.var(x, axis=-1, keepdims=True)
            return (x - m) / jnp.sqrt(v + EPS) * g + b

        def _gelu(t):
            return jax.nn.gelu(t, approximate=False)

        def _forward(x, wq, bq, wk, bk, wv, bv, wo, bo, ln1_g, ln1_b, ln2_g, ln2_b, fc1_w, fc1_b, fc2_w, fc2_b, r_ln_g, r_ln_b, r_in_w, r_in_b, r_o1_w, r_o1_b, r_o2_w, r_o2_b, r_o3_w, r_o3_b, lra_down, lra_up):
            B, N, _ = x.shape
            e = _gelu(_ln(x, r_ln_g, r_ln_b) @ r_in_w.T + r_in_b)
            g = jnp.mean(e[:, RESERVE:, :], axis=1, keepdims=True)
            f = jnp.concatenate([e, jnp.broadcast_to(g, e.shape)], axis=-1)
            h1 = _gelu(f @ r_o1_w.T + r_o1_b)
            h2 = _gelu(h1 @ r_o2_w.T + r_o2_b)
            logits = (h2 @ r_o3_w.T + r_o3_b).reshape(B, N, BS, 2)
            hard = jax.nn.one_hot(jnp.argmax(logits, axis=-1), 2, dtype=x.dtype)
            keep = jnp.broadcast_to(jnp.array([0.0, 1.0], dtype=x.dtype), hard[:, :RESERVE].shape)
            hard = hard.at[:, :RESERVE].set(keep)
            hard = jax.lax.stop_gradient(hard)
            bits = hard[..., 1]
            indices = (bits * jnp.array([2.0, 1.0], dtype=x.dtype)).sum(-1).astype(jnp.int32)
            indices = jax.lax.stop_gradient(indices)
            xa = _ln(x, ln1_g, ln1_b)
            q = (xa @ wq.T + bq).reshape(B, N, HEADS, HD).transpose(0, 2, 1, 3)
            k = (xa @ wk.T + bk).reshape(B, N, HEADS, HD).transpose(0, 2, 1, 3)
            v = (xa @ wv.T + bv).reshape(B, N, HEADS, HD).transpose(0, 2, 1, 3)
            s = jax.nn.softmax(jnp.einsum('bhqd,bhkd->bhqk', q, k) / np.float32(np.sqrt(HD)), axis=-1)
            o = jnp.einsum('bhqk,bhkd->bhqd', s, v).transpose(0, 2, 1, 3).reshape(B, N, DIM)
            o = o @ wo.T + bo
            h = x + bits[:, :, 0:1] * o
            xf = _ln(h, ln2_g, ln2_b)
            ff = _gelu(xf @ fc1_w.T + fc1_b) @ fc2_w.T + fc2_b
            out = h + bits[:, :, 1:2] * ff
            down = jnp.einsum('bnd,krd->bknr', out, lra_down)
            up = jnp.einsum('bknr,kdr->bknd', down, lra_up)
            sel = jax.nn.one_hot(indices, 3, dtype=x.dtype)
            out = out + jnp.einsum('bknd,bnk->bnd', up, sel)
            return out
        return _forward(x, wq, bq, wk, bk, wv, bv, wo, bo, ln1_g, ln1_b, ln2_g, ln2_b, fc1_w, fc1_b, fc2_w, fc2_b, r_ln_g, r_ln_b, r_in_w, r_in_b, r_o1_w, r_o1_b, r_o2_w, r_o2_b, r_o3_w, r_o3_b, lra_down, lra_up)
    h = _L0_tok_ref(x, mask_BS_i0_1, L0_tok_word_emb, L0_tok_pos_emb3, L0_tok_type_emb, L0_tok_emb_ln_g, L0_tok_emb_ln_b, L0_tok_Wq, L0_tok_bq, L0_tok_Wk, L0_tok_bk, L0_tok_Wv, L0_tok_bv, L0_tok_Wo, L0_tok_bo, L0_tok_ln1_g, L0_tok_ln1_b, L0_tok_W1, L0_tok_b1, L0_tok_W2, L0_tok_b2, L0_tok_ln2_g, L0_tok_ln2_b, L0_tok_Wg, L0_tok_bg, L0_tok_pos_emb2, L0_tok_type_emb2, L0_tok_norm_g, L0_tok_norm_b)
    h = h + _L0_attn_ref(_layernorm(h, axis=-1), L0_attn_qkv_w, L0_attn_qkv_b, L0_attn_proj_w, L0_attn_proj_b)
    h = h + _L0_ffn_ref(_layernorm(h, axis=-1), L0_ffn_wq, L0_ffn_bq, L0_ffn_wk, L0_ffn_bk, L0_ffn_wv, L0_ffn_bv, L0_ffn_wo, L0_ffn_bo, L0_ffn_ln1_g, L0_ffn_ln1_b, L0_ffn_ln2_g, L0_ffn_ln2_b, L0_ffn_fc1_w, L0_ffn_fc1_b, L0_ffn_fc2_w, L0_ffn_fc2_b, L0_ffn_r_ln_g, L0_ffn_r_ln_b, L0_ffn_r_in_w, L0_ffn_r_in_b, L0_ffn_r_o1_w, L0_ffn_r_o1_b, L0_ffn_r_o2_w, L0_ffn_r_o2_b, L0_ffn_r_o3_w, L0_ffn_r_o3_b, L0_ffn_lra_down, L0_ffn_lra_up)
    return h

_drawn_inputs = setup_inputs


def setup_inputs(seed=0):
    import zlib

    import numpy as np

    out = dict(_drawn_inputs(seed))
    spreads = {'L0_tok_emb_ln_g': (1.0, 0.2),
     'L0_tok_emb_ln_b': (0.0, 0.1),
     'L0_tok_bq': (0.0, 2.0),
     'L0_tok_bk': (0.0, 2.0),
     'L0_tok_bv': (0.0, 0.1),
     'L0_tok_bo': (0.0, 0.1),
     'L0_tok_ln1_g': (1.0, 0.2),
     'L0_tok_ln1_b': (0.0, 0.1),
     'L0_tok_b1': (0.0, 0.1),
     'L0_tok_b2': (0.0, 0.1),
     'L0_tok_ln2_g': (1.0, 0.2),
     'L0_tok_ln2_b': (0.0, 0.1),
     'L0_tok_bg': (0.0, 0.1),
     'L0_tok_norm_g': (1.0, 0.2),
     'L0_tok_norm_b': (0.0, 0.1),
     'L0_attn_qkv_b': (0.0, 0.1),
     'L0_attn_proj_b': (0.0, 0.1),
     'L0_ffn_bq': (0.0, 2.0),
     'L0_ffn_bk': (0.0, 2.0),
     'L0_ffn_bv': (0.0, 0.58),
     'L0_ffn_bo': (0.0, 0.1),
     'L0_ffn_ln1_g': (1.0, 0.6),
     'L0_ffn_ln1_b': (0.0, 0.8),
     'L0_ffn_ln2_g': (1.0, 0.6),
     'L0_ffn_ln2_b': (0.0, 0.8),
     'L0_ffn_fc1_b': (0.0, 0.512),
     'L0_ffn_fc2_b': (0.0, 0.1),
     'L0_ffn_r_ln_g': (1.0, 0.2),
     'L0_ffn_r_ln_b': (0.0, 0.1),
     'L0_ffn_r_in_b': (0.0, 0.1),
     'L0_ffn_r_o1_b': (0.0, 0.1),
     'L0_ffn_r_o2_b': (0.0, 0.1)}
    factors = {'L0_tok_Wq': 8.0,
     'L0_tok_Wk': 8.0,
     'L0_tok_pos_emb2': 4.075,
     'L0_tok_type_emb2': 3.961,
     'L0_ffn_wq': 8.0,
     'L0_ffn_wk': 8.0}
    for name, (base, spread) in spreads.items():
        noise = np.random.default_rng([zlib.crc32(name.encode()), seed]).standard_normal(out[name].shape)
        drawn = base * np.exp(spread * noise) if base else spread * noise
        out[name] = jnp.asarray(drawn.astype(out[name].dtype))
    for name, factor in factors.items():
        out[name] = (out[name] * factor).astype(out[name].dtype)
    return out
```

```python
from contextlib import ExitStack

import concourse.bass as bass
from concourse import mybir

F32 = mybir.dt.float32
I32 = mybir.dt.int32
ALU = mybir.AluOpType
ACT = mybir.ActivationFunctionType
AX = mybir.AxisListType

P = 128
H = 192
HC = H // 2
NSLOT = 3
NH = 12
DH = H // NH
FF = 768
NFC = FF // P
AH = 64
AD = NH * AH
ROWS = 64
BIG = 10000.0
EPS_TOK = 1e-12
EPS = 1e-5
TOK_SCALE = DH ** -0.5
ATT_SCALE = AH ** -0.5
RHD = 128
RANK = 64

LAG = {"E": 0, "A": 1, "B": 2, "C": 3, "D": 4}
PEEL = 5

TOK_FILLS = [("tr0", "xT", 1), ("tr1", "xT", 2),
             ("qk0", "qk", 1), ("qk1", "qk", 2), ("qk2", "qk", 3), ("v01", "v", 1), ("v2", "v", 2),
             ("c0", "cT", 1), ("c1", "cT", 2), ("y01", "z1", 1), ("y2", "z1", 2),
             ("m0", "x1T", 1), ("m1", "x1T", 2),
             ("f0", "fT", 1), ("f1", "fT", 2), ("f2", "fT", 3), ("f3", "fT", 4), ("f4", "fT", 5),
             ("f5", "fT", 6), ("o01", "z2", 1), ("o2", "z2", 2)]
FILLS = {
    "A": TOK_FILLS,
    "B": TOK_FILLS + [("g0", "gT", 1), ("g1", "gT", 2), ("u0", "gx", 1), ("u1", "gx", 2),
                      ("u2", "gx", 3), ("hs", "hsum", 1)],
    "C": [("z", "zT", 1), ("qk0", "qkT", 1), ("qk1", "qkT", 2), ("qk2", "qkT", 3), ("v0", "v", 1),
          ("v1", "v", 2), ("s0", "ex", 1), ("s1", "ex", 2), ("s2", "ex", 3), ("s3", "ex", 4),
          ("p0", "pT", 1), ("p1", "pT", 2), ("p2", "pT", 3), ("c0", "ctx", 1), ("c1", "ctx", 2),
          ("t0", "cT", 1), ("t1", "cT", 2), ("y", "h1", 1)],
    "D": [("z", "zT", 1), ("qk0", "qkT", 1), ("qk1", "qkT", 2), ("v", "v", 1), ("e", "eT", 1),
          ("s0", "ex", 1), ("s1", "ex", 2), ("s2", "ex", 3), ("s3", "ex", 4),
          ("h1", "h1T", 1), ("h2", "h2T", 1),
          ("p0", "pT", 1), ("p1", "pT", 2), ("p2", "pT", 3), ("lg", "lgs", 1), ("c", "ctx", 1),
          ("t", "cT", 1), ("y", "hd", 1), ("z2", "z2T", 1), ("f0", "fT", 1), ("f1", "fT", 2),
          ("o", "od", 1), ("ot", "oT", 1), ("dn", "dn", 1), ("dt", "dT", 1), ("up", "fin", 1)],
}
BANK0 = {"A": 0, "B": 2, "C": 4, "D": 6}

TOK_SIGNALS = dict(xT=2, qk=3, v=2, qkp=3, shifted=1, ex=1, p=1, pvp=3, ctx=1, cT=2,
                   ve1=1, rs1=1, z1=2, x1T=2, fT=6, ve2=1, rs2=1, z2=2)
SIGNALS = {
    "E": dict(idx=1, loaded=48, emb=1, ve=1, rs=1),
    "A": TOK_SIGNALS | dict(zin=1),
    "B": TOK_SIGNALS | dict(gT=2, th=3, gx=3, gm=1, hsum=1, ve3=1, rs3=1, z3=1, zg=1, h0=1,
                            h0b=1),
    "C": dict(ve=1, rs=1, z=1, zT=1, qkT=3, v=2, nm=4, ex=4, pT=3, ctx=2, cT=2, h1=1),
    "D": dict(vex=1, rsx=1, x=1, ve=1, rs=1, z=1, zT=1, zrT=1, eT=1, gs=1, hb=1, h1T=1, h2T=1,
              lgs=1, sel=1, qkT=2, v=1, nm=4, ex=4, pT=3, ctx=1, cT=1, hd=1, ve2=1, rs2=1, z2=1,
              z2T=1, fT=2, od=1, out=1, oT=1, dn=1, dT=1, fin=1, stored=16),
}
C_HEADS = [[0, 2, 4], [1, 3, 5], [6, 8, 10], [7, 9, 11]]
D_HEADS = [[r, r + 4, r + 8] for r in range(4)]

ORDER = [
    ("B", "tr"), ("D", "ln_x"), ("D", "norm_x"), ("A", "tr"), ("B", "qkv"), ("C", "ln"), ("D", "ln_z"),
    ("D", "norm_z"), ("A", "qkv"), ("B", "qkp"), ("C", "norm"), ("B", "soft"), ("D", "qk"),
    ("A", "qkp"), ("B", "pv"), ("D", "e"), ("C", "qk"), ("A", "soft"), ("B", "ctx"), ("D", "sA"),
    ("B", "tc"), ("C", "v"), ("A", "pv"), ("E", "gather"), ("D", "sB"), ("B", "y"), ("A", "ctx"),
    ("D", "h1"), ("A", "tc"), ("D", "h2"), ("B", "ln1"), ("B", "norm1"), ("A", "y"), ("D", "p"),
    ("A", "ln1"), ("B", "m"), ("C", "sA"), ("D", "lg"), ("A", "norm1"), ("D", "c"), ("B", "ff"),
    ("A", "m"), ("E", "stats"), ("D", "t"), ("B", "o"), ("D", "y"), ("D", "ln2"), ("B", "ln2"),
    ("D", "norm2"), ("A", "ff"), ("B", "norm2"), ("D", "z2"), ("B", "g"), ("C", "sB"), ("A", "o"),
    ("B", "u"), ("C", "p"), ("D", "ff"), ("C", "c"), ("A", "ln2"), ("D", "o"), ("B", "hs"), ("D", "ot"),
    ("B", "ln3"), ("A", "norm2"), ("C", "t"), ("D", "dn"), ("C", "y"), ("B", "norm3"), ("E", "norm"),
    ("D", "dt"), ("D", "up"), ("B", "h0"),
]


class Row:

    def __init__(self, turn, base, lag):
        self.turn, self.base = turn, base - lag

    def times(self, k, c):
        c += k * self.base
        if self.turn is None:
            return c
        return self.turn * k + c if c else self.turn * k


class Chain:

    def __init__(self, sem):
        self.sem, self.count, self.per_row = sem, 0, 0

    def begin(self, row):
        if self.count:
            self.per_row = self.count
        self.count = 0

    def tick(self):
        self.count += 1
        return 1

    def value(self, row):
        return row.times(self.per_row, self.count)


def build_tower(nc, d, out):
    with ExitStack() as ctx:
        def sb(name, shape, dt=F32):
            return ctx.enter_context(nc.sbuf_tensor(name, shape, dt))

        def sem(name):
            return ctx.enter_context(nc.semaphore(name))

        bank = [ctx.enter_context(nc.psum_tensor(f"bank{i}", [P, 512], F32)) for i in range(8)]
        full = [sem(f"full{i}") for i in range(8)]
        signal = {lane: {name: sem(f"{lane}_{name}") for name in SIGNALS[lane]} for lane in SIGNALS}
        weights_loaded = sem("weights_loaded")
        masks_ready = sem("masks_ready")
        const_ready = sem("const_ready")

        loads = []

        def weight(name, shape, dt=F32):
            t = sb("w_" + name, shape, dt)
            loads.append((t, name))
            return t

        ident = weight("ident", [P, P])
        shifts = weight("shifts", [P, NSLOT, P])
        wqkv = [weight(f"tok_qkv{l}", [HC + 1, 2, 3 * H]) for l in range(2)]
        wo = [weight(f"tok_o{l}", [HC, 2, H]) for l in range(2)]
        res1 = [weight(f"tok_res1{l}", [HC + 1, H]) for l in range(2)]
        res2 = [weight(f"tok_res2{l}", [HC + 1, H]) for l in range(2)]
        w1 = [weight(f"tok_w1{l}", [HC, 2, FF]) for l in range(2)]
        w2 = [weight(f"tok_w2{l}", [P, NFC, H]) for l in range(2)]
        wgate = weight("tok_gate", [HC + 1, 2, 2 * H])
        cols = weight("cols", [P, 64])
        pos3 = weight("pos3", [P, NSLOT * H])
        type0 = weight("type0", [P, H])
        pos2 = weight("pos2", [P, H])
        type2 = weight("type2", [P, 2, H])
        norm_gb = weight("norm_gb", [P, 2, H])
        proj_b = weight("proj_b", [P, H])
        fc2_b = weight("fc2_b", [P, H])
        first = weight("first", [P, 2])
        c_qkv = weight("att_qkv", [HC + 1, 2, 3 * AD])
        c_proj = weight("att_proj", [P, AD // P, H])
        d_qk = weight("ffn_qk", [HC + 1, 2, 6 * P])
        d_v = weight("ffn_v", [HC + 1, 2, H])
        d_o = weight("ffn_o", [HC + 1, 2, H])
        d_fc1 = weight("ffn_fc1", [HC, 2, FF])
        d_fc2 = weight("ffn_fc2", [P, NFC, H])
        d_rin = weight("ffn_rin", [HC, 2, RHD])
        d_ro1 = weight("ffn_ro1", [RHD, 2, RHD])
        d_ro2 = weight("ffn_ro2", [RHD, RHD // 2])
        d_ro3 = weight("ffn_ro3", [RHD // 2 + 1, 4])
        d_down = weight("ffn_down", [HC, 2, NSLOT * RANK])
        d_up = weight("ffn_up", [HC, 2, H])
        ids = weight("ids", [P, ROWS * NSLOT], I32)
        kinds = weight("kinds", [P, ROWS], I32)
        col_at = {}
        at = 0
        for name, n in COLS:
            col_at[name] = at
            at += n
        assert at <= 64

        def col(name, parts, k=0):
            c = col_at[name] + k
            return cols[0:parts, c:c + 1]

        mask = sb("mask", [P, ROWS * NSLOT])
        gate_mask = sb("gate_mask", [P, ROWS * NSLOT])
        att_bias = sb("att_bias", [P, ROWS * NSLOT])
        kind = sb("kind", [P, ROWS])
        scratch = sb("scratch", [P, 2])
        minus_half = sb("minus_half", [P, NSLOT])

        idx = sb("idx", [P, 4], I32)
        emb = sb("emb", [P, NSLOT * H])
        embsum = sb("embsum", [P, NSLOT * H])

        TOK = "AB"
        zin = {l: sb(f"{l}_zin", [P, NSLOT, H]) for l in TOK}
        xT = {l: sb(f"{l}_xT", [HC + 1, 2, NSLOT * P]) for l in TOK}
        qkv = {l: sb(f"{l}_qkv", [P, NSLOT, 3 * H]) for l in TOK}
        fT = {l: sb(f"{l}_fT", [P, NFC, NSLOT * P]) for l in TOK}
        prod = {l: fT[l][:, :, :].rearrange("p a b -> p (a b)")[:, 0:9 * H] for l in TOK}
        ctxt = {l: sb(f"{l}_ctx", [P, NSLOT, H]) for l in TOK}
        cT = {l: sb(f"{l}_cT", [HC + 1, 2, NSLOT * P]) for l in TOK}
        sc = {l: sb(f"{l}_sc", [P, NSLOT * NSLOT * NH]) for l in TOK}
        pr = {l: sb(f"{l}_pr", [P, NSLOT * NSLOT * NH]) for l in TOK}
        mx = {l: sb(f"{l}_mx", [P, NSLOT * NH]) for l in TOK}
        gated = qkv["B"][:, :, 0:H]
        tanh = qkv["B"][:, :, H:2 * H]
        hpre = sb("hpre", [P, H])
        aux = sb("aux", [P, H])
        h0 = sb("h0", [P, H])
        h0b = sb("h0b", [P, H])

        LNS = [("E", "", 3), ("A", "1", 3), ("A", "2", 3), ("B", "1", 3), ("B", "2", 3), ("B", "3", 1),
               ("C", "", 1), ("D", "x", 1), ("D", "", 1), ("D", "2", 1)]
        lnst = {(l, n): (sb(f"{l}_st{n}", [P, k, 6]), sb(f"{l}_mv{n}", [P, k, 2]),
                         sb(f"{l}_ve{n}_", [P, k]), sb(f"{l}_rs{n}_", [P, k])) for l, n, k in LNS}

        c_z = sb("C_z", [P, H])
        c_zT = sb("C_zT", [HC + 1, 2, P])
        c_qkT = sb("C_qkT", [P, NH, P])
        c_v = sb("C_v", [P, AD])
        c_p = sb("C_p", [P, NH, P])
        c_ctx = c_p[:, 0:6, :].rearrange("p a b -> p (a b)")
        c_cT = c_p[:, 6:12, :]
        c_nm = sb("C_nm", [P, 2, 12])
        c_sum = sb("C_sum", [P, 2, NH])
        h1 = sb("h1", [P, H])

        d_x = sb("D_x", [P, H])
        d_h1 = sb("D_h1", [P, H])
        d_z = sb("D_z", [P, H])
        d_zT = sb("D_zT", [HC + 1, 2, P])
        d_zrT = sb("D_zrT", [HC, 2, P])
        d_eT = sb("D_eT", [P, P])
        d_h1T = sb("D_h1T", [P, P])
        d_h2T = sb("D_h2T", [RHD // 2 + 1, P])
        d_small = sb("D_small", [P, 32])
        d_pT = sb("D_pT", [P, NH, P])
        d_qkT = d_pT[:, 0:6, :]
        d_vs = sb("D_v", [P, H])
        d_p = sb("D_p", [P, NH, P])
        d_fT = d_p[:, 0:NFC, :]
        d_nm = sb("D_nm", [P, 2, 12])
        d_sum = sb("D_sum", [P, 2, NH])
        d_ctx = sb("D_ctx", [P, H])
        d_cT = sb("D_cT", [HC + 1, 2, P])
        d_h = sb("D_h", [P, H])
        d_z2T = sb("D_z2T", [HC, 2, P])
        d_ff = d_ctx
        d_out = sb("D_out", [P, H])
        d_oT = sb("D_oT", [HC, 2, P])
        d_dn = sb("D_dn", [P, H])
        d_fin = sb("D_fin", [P, H])

        bits = d_small[:, 0:2]
        nbits = d_small[:, 2:4]
        sel = d_small[:, 4:7]
        logits = d_small[:, 8:12]
        gsum = d_small[:, 12:13]
        hbias = d_small[:, 13:14]
        gmean = d_small[:, 14:15]

        place, on_bank = {}, {b: 0 for b in range(8)}
        before = {}
        claims = dict.fromkeys(FILLS, 0)
        for lane, fills in FILLS.items():
            last = [None, None]
            for n, (fill, name, value) in enumerate(fills):
                b = BANK0[lane] + n % 2
                on_bank[b] += 1
                place[lane, fill] = (b, on_bank[b])
                before[lane, fill] = last[n % 2]
                last[n % 2] = (name, value, 0)
            for fill, *_ in fills[:2]:
                k = place[lane, fill][0] - BANK0[lane]
                before[lane, fill] = (*last[k][:2], 1)

        def made(lane, name, row, value=None, back=0):
            per = SIGNALS[lane][name]
            n = row.times(per, (per if value is None else value) - back * per)
            return reached(signal[lane][name], n)

        def written(lane, fill, row, back=0):
            b, k = place[lane, fill]
            return reached(full[b], row.times(on_bank[b], k - back * on_bank[b]))

        def drained(lane, fill, row):
            assert fill == FILLS[lane][claims[lane] % len(FILLS[lane])][0]
            claims[lane] += 1
            name, value, back = before[lane, fill]
            return made(lane, name, row, value, back)

        def reached(sem, n):
            return (const_ready, 3) if isinstance(n, int) and n <= 0 else (sem, n)

        def bank_of(lane, fill):
            return place[lane, fill][0]

        def psum(lane, fill):
            return bank[place[lane, fill][0]]

        def run(engine, steps):
            def turn(reg, base, lanes):
                rows = {lane: Row(reg, base, LAG[lane]) for lane in LAG}
                for lane in lanes:
                    for chain in steps.get("chains", {}).get(lane, ()):
                        chain.begin(rows[lane])
                for lane, step in ORDER:
                    if lane in lanes and (lane, step) in steps:
                        steps[lane, step](rows[lane])
            for t in range(PEEL):
                turn(None, t, [l for l in LAG if t >= LAG[l]])
            with engine.Fori(0, ROWS - PEEL) as reg:
                turn(reg, PEEL, list(LAG))
            for t in range(ROWS, ROWS + LAG["D"]):
                turn(None, t, [l for l in LAG if t < ROWS + LAG[l]])

        block = ctx.enter_context(nc.Block())

        @block.sync
        def _(sp):
            for t, name in loads:
                sp.dma_start(t[:], d[name]).then_inc(weights_loaded, 16)

            def store(row):
                sp.wait_ge(*made("D", "fin", row))
                sp.dma_start(out[bass.ds(row.times(P, 0), P), :], d_fin[:, :]).then_inc(signal["D"]["stored"], 16)
            run(sp, {("D", "up"): store})
            sp.wait_ge(signal["D"]["stored"], 16 * ROWS)

        @block.gpsimd
        def _(pool):
            pool.memset(minus_half[:, :], -0.5).then_inc(const_ready, 1)
            pool.wait_ge(weights_loaded, 16 * len(loads))
            pool.wait_ge(const_ready, 2)
            for j in range(NSLOT):
                last = pool.tensor_tensor(pos3[:, j * H:(j + 1) * H], pos3[:, j * H:(j + 1) * H],
                                          type0[:, :], ALU.add)
            last.then_inc(const_ready, 1)
            pool.wait_ge(const_ready, 3)

            def gather(row):
                pool.wait_ge(*made("E", "loaded", row, back=1))
                pool.tensor_copy(idx[:, 0:NSLOT], ids[:, bass.ds(row.times(NSLOT, 0), NSLOT)]
                                 ).then_inc(signal["E"]["idx"], 1)
                pool.wait_ge(*made("E", "idx", row))
                pool.wait_ge(*made("E", "emb", row, back=1))
                pool.tensor_tensor(scratch[:, 1:2], minus_half[:, 0:1], minus_half[:, 0:1], ALU.add)
                for j in range(NSLOT):
                    pool.indirect_dma_start(emb[:, j * H:(j + 1) * H], None, d["word_emb"],
                                            bass.IndirectOffsetOnAxis(idx[:, j:j + 1], 0)
                                            ).then_inc(signal["E"]["loaded"], 16)

            def add_positions(row):
                pool.wait_ge(*made("E", "loaded", row))
                pool.wait_ge(*made("A", "zin", row, back=1))
                pool.tensor_tensor(embsum[:, :], emb[:, :], pos3[:, :], ALU.add
                                   ).then_inc(signal["E"]["emb"], 1)

            def inverse_deviation(lane, n=""):
                def step(row):
                    pool.wait_ge(*made(lane, "ve" + n, row))
                    _, _, ve, rs = lnst[lane, n]
                    pool.tensor_tensor(rs[:, :], ve[:, :], minus_half[:, 0:ve.shape[1]], ALU.pow
                                       ).then_inc(signal[lane]["rs" + n], 1)
                return step

            def qk_products(lane):
                def step(row):
                    pool.wait_ge(*made(lane, "qk", row))
                    pool.wait_ge(*written(lane, "o2", row, back=1))
                    pv = prod[lane].rearrange("p (i k f) -> p i k f", i=NSLOT, k=NSLOT)
                    for i in range(NSLOT):
                        q = qkv[lane][:, i, 0:H].unsqueeze(1).to_broadcast([P, NSLOT, H])
                        pool.tensor_tensor(pv[:, i, :, :], q, qkv[lane][:, :, H:2 * H], ALU.mult
                                           ).then_inc(signal[lane]["qkp"], 1)
                return step

            def pv_products(lane):
                def step(row):
                    pool.wait_ge(*made(lane, "p", row))
                    pool.wait_ge(*made(lane, "v", row))
                    pv = prod[lane].rearrange("p (i k h d) -> p i k h d", i=NSLOT, k=NSLOT, h=NH)
                    pp = pr[lane][:, :].rearrange("p (i k h) -> p i k h", i=NSLOT, k=NSLOT)
                    for i in range(NSLOT):
                        for k in range(NSLOT):
                            v = qkv[lane][:, k, 2 * H:3 * H].rearrange("p (h d) -> p h d", h=NH)
                            w = pp[:, i, k, :].unsqueeze(2).to_broadcast([P, NH, DH])
                            last = pool.tensor_tensor(pv[:, i, k], v, w, ALU.mult)
                        last.then_inc(signal[lane]["pvp"], 1)
                return step

            def add_proj_bias(row):
                pool.wait_ge(*made("B", "h0", row))
                pool.wait_ge(*made("C", "h1", row, back=1))
                pool.tensor_tensor(h0b[:, :], h0[:, :], proj_b[:, :], ALU.add
                                   ).then_inc(signal["B"]["h0b"], 1)

            steps = {("E", "gather"): gather, ("E", "stats"): None, ("B", "h0"): add_proj_bias}

            def emb_step(row):
                add_positions(row)
            steps["E", "stats"] = emb_step
            steps["E", "norm"] = inverse_deviation("E")
            for l in TOK:
                steps[l, "qkp"] = qk_products(l)
                steps[l, "pv"] = pv_products(l)
                steps[l, "ln1"] = inverse_deviation(l, "1")
                steps[l, "ln2"] = inverse_deviation(l, "2")
            steps["B", "ln3"] = inverse_deviation("B", "3")
            steps["C", "ln"] = inverse_deviation("C")
            steps["D", "ln_x"] = inverse_deviation("D", "x")
            steps["D", "ln_z"] = inverse_deviation("D")
            steps["D", "ln2"] = inverse_deviation("D", "2")
            run(pool, steps)

        @block.tensor
        def _(pe):
            pe.wait_ge(weights_loaded, 16 * len(loads))
            pe.wait_ge(const_ready, 3)

            def transpose_slots(lane, row, src, fills):
                for c, fill in enumerate(fills):
                    pe.wait_ge(*drained(lane, fill, row))
                    dst = psum(lane, fill)
                    for j in range(NSLOT):
                        last = pe.transpose(dst[0:HC, j * P:(j + 1) * P], src[:, j, c * HC:(c + 1) * HC], ident[:, :])
                    last.then_inc(full[bank_of(lane, fill)], 1)

            def transpose_pair(lane, row, src, fill):
                pe.wait_ge(*drained(lane, fill, row))
                dst = psum(lane, fill)
                for c in range(2):
                    last = pe.transpose(dst[0:HC, c * P:(c + 1) * P], src[:, c * HC:(c + 1) * HC], ident[:, :])
                last.then_inc(full[bank_of(lane, fill)], 1)

            def tok_tr(lane):
                def step(row):
                    pe.wait_ge(*made("A", "zin" if lane == "A" else "z2", row))
                    transpose_slots(lane, row, zin[lane], ("tr0", "tr1"))
                return step

            def tok_qkv(lane, l):
                def step(row):
                    pe.wait_ge(*made(lane, "xT", row))
                    w = wqkv[l]
                    x = xT[lane]
                    for j in range(NSLOT):
                        pe.wait_ge(*drained(lane, f"qk{j}", row))
                        dst = psum(lane, f"qk{j}")
                        tok = slice(j * P, (j + 1) * P)
                        pe.matmul(dst[:, 0:2 * H], x[0:HC, 0, tok], w[0:HC, 0, 0:2 * H], start=True, stop=False)
                        pe.matmul(dst[:, 0:2 * H], x[:, 1, tok], w[:, 1, 0:2 * H],
                                                        start=False, stop=True).then_inc(full[bank_of(lane, f"qk{j}")], 1)
                    for fill, slots in (("v01", (0, 1)), ("v2", (2,))):
                        pe.wait_ge(*drained(lane, fill, row))
                        dst = psum(lane, fill)
                        for n, j in enumerate(slots):
                            tok = slice(j * P, (j + 1) * P)
                            o = dst[:, n * H:(n + 1) * H]
                            pe.matmul(o, x[0:HC, 0, tok], w[0:HC, 0, 2 * H:], start=True, stop=False)
                            last = pe.matmul(o, x[:, 1, tok], w[:, 1, 2 * H:], start=False, stop=True)
                        last.then_inc(full[bank_of(lane, fill)], 1)
                return step

            def tok_tc(lane):
                def step(row):
                    pe.wait_ge(*made(lane, "ctx", row))
                    transpose_slots(lane, row, ctxt[lane], ("c0", "c1"))
                return step

            def residual(o, xT_, tok, res):
                pe.matmul(o[:, 0:HC], xT_[0:HC, 0, tok], ident[0:HC, 0:HC], start=False, stop=False)
                return pe.matmul(o, xT_[:, 1, tok], res[:, :], start=False, stop=True)

            def tok_y(lane, l):
                def step(row):
                    pe.wait_ge(*made(lane, "cT", row))
                    for fill, slots in (("y01", (0, 1)), ("y2", (2,))):
                        pe.wait_ge(*drained(lane, fill, row))
                        dst = psum(lane, fill)
                        for n, j in enumerate(slots):
                            tok = slice(j * P, (j + 1) * P)
                            o = dst[:, n * H:(n + 1) * H]
                            pe.matmul(o, cT[lane][0:HC, 0, tok], wo[l][:, 0, :], start=True, stop=False)
                            pe.matmul(o, cT[lane][0:HC, 1, tok], wo[l][:, 1, :], start=False, stop=False)
                            last = residual(o, xT[lane], tok, res1[l])
                        last.then_inc(full[bank_of(lane, fill)], 1)
                return step

            def tok_m(lane):
                def step(row):
                    pe.wait_ge(*made(lane, "z1", row))
                    transpose_slots(lane, row, ctxt[lane], ("m0", "m1"))
                return step

            def tok_ff(lane, l):
                def step(row):
                    pe.wait_ge(*made(lane, "x1T", row))
                    for f in range(NFC):
                        pe.wait_ge(*drained(lane, f"f{f}", row))
                        dst = psum(lane, f"f{f}")
                        fs = slice(f * P, (f + 1) * P)
                        pe.matmul(dst[:, 0:NSLOT * P], w1[l][:, 0, fs], cT[lane][0:HC, 0, :], start=True, stop=False)
                        pe.matmul(dst[:, 0:NSLOT * P], w1[l][:, 1, fs], cT[lane][0:HC, 1, :],
                                                       start=False, stop=True).then_inc(full[bank_of(lane, f"f{f}")], 1)
                return step

            def tok_o(lane, l):
                def step(row):
                    pe.wait_ge(*made(lane, "fT", row))
                    for fill, slots in (("o01", (0, 1)), ("o2", (2,))):
                        pe.wait_ge(*drained(lane, fill, row))
                        dst = psum(lane, fill)
                        for n, j in enumerate(slots):
                            tok = slice(j * P, (j + 1) * P)
                            o = dst[:, n * H:(n + 1) * H]
                            for f in range(NFC):
                                pe.matmul(o, fT[lane][:, f, tok], w2[l][:, f, :], start=(f == 0), stop=False)
                            last = residual(o, cT[lane], tok, res2[l])
                        last.then_inc(full[bank_of(lane, fill)], 1)
                return step

            def gate_tr(row):
                pe.wait_ge(*made("B", "z2", row))
                transpose_slots("B", row, ctxt["B"], ("g0", "g1"))

            def gate(row):
                pe.wait_ge(*made("B", "gT", row))
                for j in range(NSLOT):
                    pe.wait_ge(*drained("B", f"u{j}", row))
                    dst = psum("B", f"u{j}")
                    tok = slice(j * P, (j + 1) * P)
                    pe.matmul(dst[:, 0:2 * H], xT["B"][0:HC, 0, tok], wgate[0:HC, 0, :], start=True, stop=False)
                    pe.matmul(dst[:, 0:2 * H], xT["B"][:, 1, tok], wgate[:, 1, :],
                                                  start=False, stop=True).then_inc(full[bank_of("B", f"u{j}")], 1)

            def window_sum(row):
                pe.wait_ge(*made("B", "gm", row))
                pe.wait_ge(*drained("B", "hs", row))
                dst = psum("B", "hs")
                for n, j in enumerate((1, 0, 2)):
                    last = pe.matmul(dst[:, 0:H], shifts[:, j, :], gated[:, j, :], start=(n == 0), stop=(n == 2))
                last.then_inc(full[bank_of("B", "hs")], 1)

            def c_qk(row):
                pe.wait_ge(*made("C", "z", row))
                transpose_pair("C", row, c_z, "z")
                pe.wait_ge(*made("C", "zT", row))
                for g in range(3):
                    pe.wait_ge(*drained("C", f"qk{g}", row))
                    dst = psum("C", f"qk{g}")
                    for k in range(4):
                        m = 4 * g + k
                        o = dst[:, k * P:(k + 1) * P]
                        ws = slice(m * P, (m + 1) * P)
                        pe.matmul(o, c_qkv[0:HC, 0, ws], c_zT[0:HC, 0, :], start=True, stop=False)
                        last = pe.matmul(o, c_qkv[:, 1, ws], c_zT[:, 1, :], start=False, stop=True)
                    last.then_inc(full[bank_of("C", f"qk{g}")], 1)

            def c_values(row):
                for g in range(2):
                    pe.wait_ge(*drained("C", f"v{g}", row))
                    dst = psum("C", f"v{g}")
                    ws = slice(2 * AD + g * 384, 2 * AD + (g + 1) * 384)
                    pe.matmul(dst[:, 0:384], c_zT[0:HC, 0, :], c_qkv[0:HC, 0, ws], start=True, stop=False)
                    pe.matmul(dst[:, 0:384], c_zT[:, 1, :], c_qkv[:, 1, ws],
                                                  start=False, stop=True).then_inc(full[bank_of("C", f"v{g}")], 1)

            def c_scores(fills):
                def step(row):
                    pe.wait_ge(*made("C", "qkT", row))
                    for f in fills:
                        pe.wait_ge(*drained("C", f"s{f}", row))
                        dst = psum("C", f"s{f}")
                        for n, h in enumerate(C_HEADS[f]):
                            r = slice(AH * (h % 2), AH * (h % 2) + AH)
                            last = pe.matmul(dst[:, n * P:(n + 1) * P], c_qkT[r, h // 2, :], c_qkT[r, 6 + h // 2, :],
                                             start=True, stop=True)
                        last.then_inc(full[bank_of("C", f"s{f}")], 1)
                return step

            def transpose_p(lane, probs):
                def step(row):
                    pe.wait_ge(*made(lane, "ex", row))
                    for g in range(3):
                        pe.wait_ge(*drained(lane, f"p{g}", row))
                        dst = psum(lane, f"p{g}")
                        for k in range(4):
                            last = pe.transpose(dst[:, k * P:(k + 1) * P], probs[:, 4 * g + k, :], ident[:, :])
                        last.then_inc(full[bank_of(lane, f"p{g}")], 1)
                return step

            def c_context(row):
                pe.wait_ge(*made("C", "pT", row))
                pe.wait_ge(*made("C", "v", row))
                for g in range(2):
                    pe.wait_ge(*drained("C", f"c{g}", row))
                    dst = psum("C", f"c{g}")
                    for k in range(6):
                        h = 6 * g + k
                        last = pe.matmul(dst[:, k * AH:(k + 1) * AH], c_qkT[:, h, :], c_v[:, h * AH:(h + 1) * AH],
                                         start=True, stop=True)
                    last.then_inc(full[bank_of("C", f"c{g}")], 1)

            def c_tr(row):
                pe.wait_ge(*made("C", "ctx", row))
                for g in range(2):
                    pe.wait_ge(*drained("C", f"t{g}", row))
                    dst = psum("C", f"t{g}")
                    for k in range(3):
                        m = 3 * g + k
                        last = pe.transpose(dst[:, k * P:(k + 1) * P], c_ctx[:, m * P:(m + 1) * P], ident[:, :])
                    last.then_inc(full[bank_of("C", f"t{g}")], 1)

            def c_out(row):
                pe.wait_ge(*made("C", "cT", row))
                pe.wait_ge(*drained("C", "y", row))
                dst = psum("C", "y")
                for m in range(6):
                    last = pe.matmul(dst[:, 0:H], c_cT[:, m, :], c_proj[:, m, :], start=(m == 0), stop=(m == 5))
                last.then_inc(full[bank_of("C", "y")], 1)

            def d_qkv(row):
                pe.wait_ge(*made("D", "z", row))
                transpose_pair("D", row, d_z, "z")

            def router_e(row):
                pe.wait_ge(*made("D", "zrT", row))
                pe.wait_ge(*drained("D", "e", row))
                dst = psum("D", "e")
                for c in range(2):
                    last = pe.matmul(dst[:, 0:P], d_rin[:, c, :], d_zrT[:, c, :], start=(c == 0), stop=(c == 1))
                last.then_inc(full[bank_of("D", "e")], 1)

            def router_h1(row):
                pe.wait_ge(*made("D", "gs", row))
                pe.wait_ge(*drained("D", "h1", row))
                dst = psum("D", "h1")
                pe.matmul(dst[:, 0:P], d_ro1[:, 0, :], d_eT[:, :], start=True, stop=True)
                pe.matmul(dst[:, P:P + 1], d_ro1[:, 1, :], gmean, start=True, stop=True).then_inc(full[bank_of("D", "h1")], 1)

            def router_h2(row):
                pe.wait_ge(*made("D", "h1T", row))
                pe.wait_ge(*drained("D", "h2", row))
                dst = psum("D", "h2")
                pe.matmul(dst[0:RHD // 2, 0:P], d_ro2[:, :], d_h1T[:, :], start=True, stop=True).then_inc(full[bank_of("D", "h2")], 1)

            def router_logits(row):
                pe.wait_ge(*made("D", "h2T", row))
                pe.wait_ge(*drained("D", "lg", row))
                dst = psum("D", "lg")
                pe.matmul(dst[:, 0:4], d_h2T[:, :], d_ro3[:, :], start=True, stop=True).then_inc(full[bank_of("D", "lg")], 1)

            def d_heads(row):
                pe.wait_ge(*made("D", "zT", row))
                for g in range(2):
                    pe.wait_ge(*drained("D", f"qk{g}", row))
                    dst = psum("D", f"qk{g}")
                    for k in range(3):
                        m = 3 * g + k
                        o = dst[:, k * P:(k + 1) * P]
                        ws = slice(m * P, (m + 1) * P)
                        pe.matmul(o, d_qk[0:HC, 0, ws], d_zT[0:HC, 0, :], start=True, stop=False)
                        last = pe.matmul(o, d_qk[:, 1, ws], d_zT[:, 1, :], start=False, stop=True)
                    last.then_inc(full[bank_of("D", f"qk{g}")], 1)
                pe.wait_ge(*drained("D", "v", row))
                dst = psum("D", "v")
                pe.matmul(dst[:, 0:H], d_zT[0:HC, 0, :], d_v[0:HC, 0, :], start=True, stop=False)
                pe.matmul(dst[:, 0:H], d_zT[:, 1, :], d_v[:, 1, :], start=False, stop=True).then_inc(full[bank_of("D", "v")], 1)

            def d_scores(fills):
                def step(row):
                    pe.wait_ge(*made("D", "qkT", row))
                    for f in fills:
                        pe.wait_ge(*drained("D", f"s{f}", row))
                        dst = psum("D", f"s{f}")
                        for n, h in enumerate(D_HEADS[f]):
                            r = slice(32 * (h % 4), 32 * (h % 4) + DH)
                            last = pe.matmul(dst[:, n * P:(n + 1) * P], d_qkT[r, h // 4, :], d_qkT[r, 3 + h // 4, :],
                                             start=True, stop=True)
                        last.then_inc(full[bank_of("D", f"s{f}")], 1)
                return step

            def d_context(row):
                pe.wait_ge(*made("D", "pT", row))
                pe.wait_ge(*made("D", "v", row))
                pe.wait_ge(*drained("D", "c", row))
                dst = psum("D", "c")
                for h in range(NH):
                    last = pe.matmul(dst[:, h * DH:(h + 1) * DH], d_pT[:, h, :], d_vs[:, h * DH:(h + 1) * DH],
                                     start=True, stop=True)
                last.then_inc(full[bank_of("D", "c")], 1)

            def d_tr(src, needs, fill):
                def step(row):
                    pe.wait_ge(*made("D", needs, row))
                    transpose_pair("D", row, src, fill)
                return step

            def pair_product(lhs, w, needs, fill):
                def step(row):
                    pe.wait_ge(*made("D", needs, row))
                    pe.wait_ge(*drained("D", fill, row))
                    dst = psum("D", fill)
                    pe.matmul(dst[:, 0:H], lhs[0:HC, 0, :], w[0:HC, 0, :], start=True, stop=False)
                    pe.matmul(dst[:, 0:H], lhs[:, 1, :], w[:, 1, :], start=False, stop=True).then_inc(full[bank_of("D", fill)], 1)
                return step

            def d_hidden(row):
                pe.wait_ge(*made("D", "z2T", row))
                for g in range(2):
                    pe.wait_ge(*drained("D", f"f{g}", row))
                    dst = psum("D", f"f{g}")
                    for k in range(3):
                        fs = slice((3 * g + k) * P, (3 * g + k + 1) * P)
                        o = dst[:, k * P:(k + 1) * P]
                        pe.matmul(o, d_fc1[:, 0, fs], d_z2T[:, 0, :], start=True, stop=False)
                        last = pe.matmul(o, d_fc1[:, 1, fs], d_z2T[:, 1, :], start=False, stop=True)
                    last.then_inc(full[bank_of("D", f"f{g}")], 1)

            def d_mlp_out(row):
                pe.wait_ge(*made("D", "fT", row))
                pe.wait_ge(*drained("D", "o", row))
                dst = psum("D", "o")
                for f in range(NFC):
                    last = pe.matmul(dst[:, 0:H], d_fT[:, f, :], d_fc2[:, f, :], start=(f == 0), stop=(f == NFC - 1))
                last.then_inc(full[bank_of("D", "o")], 1)

            steps = {}
            for l, lane in enumerate(TOK):
                steps[lane, "tr"] = tok_tr(lane)
                steps[lane, "qkv"] = tok_qkv(lane, l)
                steps[lane, "tc"] = tok_tc(lane)
                steps[lane, "y"] = tok_y(lane, l)
                steps[lane, "m"] = tok_m(lane)
                steps[lane, "ff"] = tok_ff(lane, l)
                steps[lane, "o"] = tok_o(lane, l)
            steps |= {("B", "g"): gate_tr, ("B", "u"): gate, ("B", "hs"): window_sum,
                      ("C", "qk"): c_qk, ("C", "v"): c_values, ("C", "sA"): c_scores((0, 1)),
                      ("C", "sB"): c_scores((2, 3)), ("C", "p"): transpose_p("C", c_p),
                      ("C", "c"): c_context, ("C", "t"): c_tr, ("C", "y"): c_out,
                      ("D", "norm_z"): d_qkv, ("D", "e"): router_e, ("D", "h1"): router_h1,
                      ("D", "h2"): router_h2, ("D", "lg"): router_logits, ("D", "qk"): d_heads,
                      ("D", "sA"): d_scores((0, 1)), ("D", "sB"): d_scores((2, 3)),
                      ("D", "p"): transpose_p("D", d_p), ("D", "c"): d_context,
                      ("D", "t"): d_tr(d_ctx, "ctx", "t"), ("D", "y"): pair_product(d_cT, d_o, "cT", "y"),
                      ("D", "z2"): d_tr(d_z, "z2", "z2"), ("D", "ff"): d_hidden, ("D", "o"): d_mlp_out,
                      ("D", "ot"): d_tr(d_out, "out", "ot"), ("D", "dn"): pair_product(d_oT, d_down, "oT", "dn"),
                      ("D", "dt"): d_tr(d_dn, "dn", "dt"), ("D", "up"): pair_product(d_oT, d_up, "dT", "up")}
            run(pe, steps)

        @block.scalar
        def _(act):
            act.wait_ge(weights_loaded, 16 * len(loads))
            act.wait_ge(const_ready, 3)

            def scale_rows(lane, row, dst, fills, name, g, b):
                for c, fill in enumerate(fills):
                    act.wait_ge(*written(lane, fill, row))
                    act.activation(dst[0:HC, c, :], psum(lane, fill)[0:HC, 0:NSLOT * P], ACT.Identity,
                                                    bias=col(b, HC, c), scale=col(g, HC, c)).then_inc(signal[lane][name], 1)

            def tok_tr(lane, g, b):
                def step(row):
                    act.wait_ge(*written(lane, "y2", row, back=1))
                    if lane == "B":
                        act.wait_ge(*written("B", "u2", row, back=1))
                    scale_rows(lane, row, xT[lane], ("tr0", "tr1"), "xT", g, b)
                return step

            def tok_qkv(lane):
                def step(row):
                    act.wait_ge(*made(lane, "qkp", row, back=1))
                    act.wait_ge(*made(lane, "pvp", row, back=1))
                    if lane == "B":
                        act.wait_ge(*written("B", "hs", row, back=1))
                    for j in range(NSLOT):
                        act.wait_ge(*written(lane, f"qk{j}", row))
                        act.copy(qkv[lane][:, j, 0:2 * H], psum(lane, f"qk{j}")[:, 0:2 * H]).then_inc(signal[lane]["qk"], 1)
                    act.wait_ge(*written(lane, "v01", row))
                    act.copy(qkv[lane][:, 0:2, 2 * H:], psum(lane, "v01")[:, 0:2 * H]
                                             .rearrange("p (j f) -> p j f", j=2)).then_inc(signal[lane]["v"], 1)
                    act.wait_ge(*written(lane, "v2", row))
                    act.copy(qkv[lane][:, 2, 2 * H:], psum(lane, "v2")[:, 0:H]).then_inc(signal[lane]["v"], 1)
                return step

            def tok_exp(lane):
                def step(row):
                    act.wait_ge(*made(lane, "shifted", row))
                    act.activation(pr[lane][:, :], sc[lane][:, :], ACT.Exp).then_inc(signal[lane]["ex"], 1)
                return step

            def tok_tc(lane):
                def step(row):
                    act.wait_ge(*written(lane, "o2", row, back=1))
                    for c in range(2):
                        act.wait_ge(*written(lane, f"c{c}", row))
                        act.copy(cT[lane][0:HC, c, :], psum(lane, f"c{c}")[0:HC, 0:NSLOT * P]).then_inc(signal[lane]["cT"], 1)
                return step

            def tok_m(lane, l):
                def step(row):
                    act.wait_ge(*written(lane, "y2", row))
                    scale_rows(lane, row, cT[lane], ("m0", "m1"), "x1T", f"ln1_g{l}", f"ln1_b{l}")
                return step

            def tok_ff(lane, l):
                def step(row):
                    for f in range(NFC):
                        act.wait_ge(*written(lane, f"f{f}", row))
                        act.activation(fT[lane][:, f, :], psum(lane, f"f{f}")[:, 0:NSLOT * P],
                                                        ACT.Gelu, bias=col(f"b1{l}", P, f)).then_inc(signal[lane]["fT"], 1)
                return step

            def gate_tr(row):
                act.wait_ge(*written("B", "o2", row))
                scale_rows("B", row, xT["B"], ("g0", "g1"), "gT", "ln2_g1", "ln2_b1")

            def gate_tanh(row):
                for j in range(NSLOT):
                    act.wait_ge(*written("B", f"u{j}", row))
                    act.activation(tanh[:, j, :], psum("B", f"u{j}")[:, 0:H], ACT.Tanh, scale=0.5).then_inc(signal["B"]["th"], 1)

            def c_qk(row):
                act.wait_ge(*written("C", "z", row))
                act.wait_ge(*written("C", "v1", row, back=1))
                act.copy(c_zT[0:HC, :, :], psum("C", "z")[0:HC, 0:2 * P].rearrange("p (c t) -> p c t", c=2)).then_inc(signal["C"]["zT"], 1)
                act.wait_ge(*written("C", "c1", row, back=1))
                for g in range(3):
                    act.wait_ge(*written("C", f"qk{g}", row))
                    act.copy(c_qkT[:, 4 * g:4 * g + 4, :], psum("C", f"qk{g}")[:, :]
                                              .rearrange("p (k t) -> p k t", k=4)).then_inc(signal["C"]["qkT"], 1)

            def c_values(row):
                for g in range(2):
                    act.wait_ge(*written("C", f"v{g}", row))
                    act.copy(c_v[:, g * 384:(g + 1) * 384], psum("C", f"v{g}")[:, 0:384]).then_inc(signal["C"]["v"], 1)

            def exps(lane, fills, heads, probs, nm, sums, scale):
                def step(row):
                    if fills[0] == 0:
                        act.wait_ge(*written(lane, "y", row, back=1))
                        if lane == "D":
                            act.wait_ge(*written(lane, "o", row, back=1))
                    for f in fills:
                        act.wait_ge(*made(lane, "nm", row, f + 1))
                        for n, h in enumerate(heads[f]):
                            last = act.activation(probs[:, h, :], psum(lane, f"s{f}")[:, n * P:(n + 1) * P], ACT.Exp,
                                                  scale=scale, bias=nm[:, 1, 3 * f + n:3 * f + n + 1],
                                                  accum_out=sums[:, 0, h:h + 1])
                        last.then_inc(signal[lane]["ex"], 1)
                return step

            def copy_pT(lane, dst):
                def step(row):
                    for g in range(3):
                        act.wait_ge(*written(lane, f"p{g}", row))
                        act.copy(dst[:, 4 * g:4 * g + 4, :], psum(lane, f"p{g}")[:, :]
                                                  .rearrange("p (k t) -> p k t", k=4)).then_inc(signal[lane]["pT"], 1)
                return step

            def c_tr(row):
                for g in range(2):
                    act.wait_ge(*written("C", f"t{g}", row))
                    act.copy(c_cT[:, 3 * g:3 * g + 3, :], psum("C", f"t{g}")[:, 0:384]
                                             .rearrange("p (k t) -> p k t", k=3)).then_inc(signal["C"]["cT"], 1)

            def d_norm_z(row):
                act.wait_ge(*written("D", "z", row))
                act.wait_ge(*written("D", "e", row, back=1))
                act.wait_ge(*written("D", "v", row, back=1))
                for c in range(2):
                    last = act.activation(d_zrT[:, c, :], psum("D", "z")[0:HC, c * P:(c + 1) * P], ACT.Identity,
                                          bias=col("r_b", HC, c), scale=col("r_g", HC, c))
                last.then_inc(signal["D"]["zrT"], 1)
                for c in range(2):
                    last = act.activation(d_zT[0:HC, c, :], psum("D", "z")[0:HC, c * P:(c + 1) * P], ACT.Identity,
                                          bias=col("a_b", HC, c), scale=col("a_g", HC, c))
                last.then_inc(signal["D"]["zT"], 1)

            def router_e(row):
                act.wait_ge(*written("D", "e", row))
                act.wait_ge(*written("D", "h1", row, back=1))
                act.activation(d_eT[:, :], psum("D", "e")[:, 0:P], ACT.Gelu, bias=col("r_in_b", P)).then_inc(signal["D"]["eT"], 1)

            def router_h1(row):
                act.wait_ge(*made("D", "hb", row))
                act.wait_ge(*written("D", "h2", row, back=1))
                act.activation(d_h1T[:, :], psum("D", "h1")[:, 0:P], ACT.Gelu, bias=hbias).then_inc(signal["D"]["h1T"], 1)

            def router_h2(row):
                act.wait_ge(*written("D", "h2", row))
                act.wait_ge(*written("D", "lg", row, back=1))
                act.activation(d_h2T[0:RHD // 2, :], psum("D", "h2")[0:RHD // 2, 0:P], ACT.Gelu,
                                                bias=col("r_o2_b", RHD // 2)).then_inc(signal["D"]["h2T"], 1)

            def d_heads(row):
                act.wait_ge(*written("D", "c", row, back=1))
                for g in range(2):
                    act.wait_ge(*written("D", f"qk{g}", row))
                    act.copy(d_qkT[:, 3 * g:3 * g + 3, :], psum("D", f"qk{g}")[:, 0:384]
                                              .rearrange("p (k t) -> p k t", k=3)).then_inc(signal["D"]["qkT"], 1)
                act.wait_ge(*written("D", "v", row))
                act.copy(d_vs[:, :], psum("D", "v")[:, 0:H]).then_inc(signal["D"]["v"], 1)

            def copy_pair(fill, dst, name, after):
                def step(row):
                    act.wait_ge(*written("D", fill, row))
                    act.wait_ge(*written("D", after, row, back=1))
                    act.copy(dst[0:HC, :, :], psum("D", fill)[0:HC, 0:2 * P]
                                             .rearrange("p (c t) -> p c t", c=2)).then_inc(signal["D"][name], 1)
                return step

            def d_z2(row):
                act.wait_ge(*written("D", "z2", row))
                for c in range(2):
                    last = act.activation(d_z2T[:, c, :], psum("D", "z2")[0:HC, c * P:(c + 1) * P], ACT.Identity,
                                          bias=col("f_b", HC, c), scale=col("f_g", HC, c))
                last.then_inc(signal["D"]["z2T"], 1)

            def d_hidden(row):
                for g in range(2):
                    act.wait_ge(*written("D", f"f{g}", row))
                    for k in range(3):
                        last = act.activation(d_fT[:, 3 * g + k, :], psum("D", f"f{g}")[:, k * P:(k + 1) * P], ACT.Gelu,
                                              bias=col("fc1_b", P, 3 * g + k))
                    last.then_inc(signal["D"]["fT"], 1)

            steps = {}
            for l, lane in enumerate(TOK):
                g, b = (("emb_g", "emb_b"), ("ln2_g0", "ln2_b0"))[l]
                steps[lane, "tr"] = tok_tr(lane, g, b)
                steps[lane, "qkv"] = tok_qkv(lane)
                steps[lane, "soft"] = tok_exp(lane)
                steps[lane, "tc"] = tok_tc(lane)
                steps[lane, "m"] = tok_m(lane, l)
                steps[lane, "ff"] = tok_ff(lane, l)
            steps |= {("B", "g"): gate_tr, ("B", "u"): gate_tanh, ("C", "qk"): c_qk, ("C", "v"): c_values,
                      ("C", "sA"): exps("C", (0, 1), C_HEADS, c_p, c_nm, c_sum, ATT_SCALE),
                      ("C", "sB"): exps("C", (2, 3), C_HEADS, c_p, c_nm, c_sum, ATT_SCALE),
                      ("C", "p"): copy_pT("C", c_qkT), ("C", "t"): c_tr,
                      ("D", "norm_z"): d_norm_z, ("D", "e"): router_e, ("D", "h1"): router_h1,
                      ("D", "h2"): router_h2, ("D", "qk"): d_heads,
                      ("D", "sA"): exps("D", (0, 1), D_HEADS, d_p, d_nm, d_sum, TOK_SCALE),
                      ("D", "sB"): exps("D", (2, 3), D_HEADS, d_p, d_nm, d_sum, TOK_SCALE),
                      ("D", "p"): copy_pT("D", d_pT), ("D", "t"): copy_pair("t", d_cT, "cT", "y"),
                      ("D", "z2"): d_z2, ("D", "ff"): d_hidden,
                      ("D", "ot"): copy_pair("ot", d_oT, "oT", "up"), ("D", "dt"): copy_pair("dt", d_oT, "dT", "dn")}
            run(act, steps)

        @block.vector
        def _(dve):
            chains = {lane: Chain(sem(f"{lane}_dve_chain")) for lane in LAG}
            for l in TOK:
                dve.memset(xT[l][HC:HC + 1, :, :], 1.0)
                dve.memset(cT[l][HC:HC + 1, :, :], 1.0)
            for t in (c_zT, d_zT, d_cT):
                dve.memset(t[HC:HC + 1, :, :], 1.0)
            dve.memset(d_h2T[RHD // 2:RHD // 2 + 1, :], 1.0).then_inc(const_ready, 1)
            dve.wait_ge(weights_loaded, 16 * len(loads))
            dve.wait_ge(const_ready, 3)
            dve.tensor_scalar(mask[:, :], ids[:, :], 0.0, None, ALU.is_gt).then_inc(masks_ready, 1)
            dve.tensor_copy(kind[:, :], kinds[:, :]).then_inc(masks_ready, 1)
            dve.tensor_tensor(pos2[:, :], pos2[:, :], type2[:, 0, :], ALU.add).then_inc(masks_ready, 1)
            dve.tensor_tensor(type2[:, 1, :], type2[:, 1, :], type2[:, 0, :], ALU.subtract).then_inc(masks_ready, 1)
            dve.wait_ge(masks_ready, 4)
            m3 = mask[:, :].rearrange("p (r j) -> p r j", j=NSLOT)
            g3 = gate_mask[:, :].rearrange("p (r j) -> p r j", j=NSLOT)
            b3 = att_bias[:, :].rearrange("p (r j) -> p r j", j=NSLOT)
            dve.tensor_scalar(g3[:, :, 1], m3[:, :, 1], 0.5, None, ALU.mult).then_inc(masks_ready, 1)
            dve.tensor_scalar(b3[:, :, 1], m3[:, :, 1], 0.0, None, ALU.mult).then_inc(masks_ready, 1)
            for j in (0, 2):
                dve.tensor_scalar(b3[:, :, j], m3[:, :, j], BIG, -BIG, ALU.mult, ALU.add).then_inc(masks_ready, 1)
            dve.wait_ge(masks_ready, 8)
            for j in (0, 2):
                dve.tensor_tensor(g3[:, :, j], m3[:, :, j], g3[:, :, 1], ALU.mult).then_inc(masks_ready, 1)
            dve.wait_ge(masks_ready, 10)

            def statistics(lane, n, row, sources, eps):
                st, mv, ve, _ = lnst[lane, n]
                chain = chains[lane]
                for k, y in enumerate(sources):
                    dve.bn_stats(st[:, k, :], y).then_inc(chain.sem, chain.tick())
                for k in range(len(sources)):
                    if k == 0:
                        dve.wait_ge(chain.sem, chain.value(row))
                        dve.memset(scratch[:, 0:1], 0.0)
                    dve.bn_aggr(mv[:, k, :], st[:, k, :]).then_inc(chain.sem, chain.tick())
                dve.wait_ge(chain.sem, chain.value(row))
                dve.tensor_scalar(ve[:, :], mv[:, :, 1], eps, None, ALU.add).then_inc(signal[lane]["ve" + n], 1)

            def normalize(lane, n, k, dst, src):
                _, mv, _, rs = lnst[lane, n]
                return dve.tensor_scalar(dst, src, mv[:, k, 0:1], rs[:, k:k + 1], ALU.subtract, ALU.mult)

            def emb_stats(row):
                dve.wait_ge(*made("E", "emb", row))
                statistics("E", "", row, [embsum[:, j * H:(j + 1) * H] for j in range(NSLOT)], EPS_TOK)

            def emb_norm(row):
                dve.wait_ge(*made("E", "rs", row))
                dve.wait_ge(*written("A", "tr1", row, back=1))
                for j in range(NSLOT):
                    last = normalize("E", "", j, zin["A"][:, j, :], embsum[:, j * H:(j + 1) * H])
                last.then_inc(signal["A"]["zin"], 1)

            def tok_soft(lane):
                chain = chains[lane]

                def step(row):
                    pv = prod[lane].rearrange("p (i m d) -> p i m d", i=NSLOT, d=DH)
                    s = sc[lane][:, :].rearrange("p (i m) -> p i m", i=NSLOT)
                    dve.wait_ge(*made(lane, "ctx", row, back=1))
                    for i in range(NSLOT):
                        dve.wait_ge(*made(lane, "qkp", row, i + 1))
                        dve.tensor_reduce(s[:, i, :], pv[:, i], AX.X, ALU.add).then_inc(chain.sem, chain.tick())
                    dve.wait_ge(chain.sem, chain.value(row))
                    s4 = sc[lane][:, :].rearrange("p (i k h) -> p i k h", i=NSLOT, k=NSLOT)
                    for k in range(NSLOT):
                        bias = att_bias[:, bass.ds(row.times(NSLOT, k), 1)]
                        dve.tensor_scalar(s4[:, :, k, :], s4[:, :, k, :], TOK_SCALE, bias, ALU.mult, ALU.add).then_inc(chain.sem, chain.tick())
                    dve.wait_ge(chain.sem, chain.value(row))
                    m = mx[lane][:, :].rearrange("p (i h) -> p i h", i=NSLOT)
                    dve.tensor_reduce(m, s4.rearrange("p i k h -> p i h k"), AX.X, ALU.max).then_inc(chain.sem, chain.tick())
                    dve.wait_ge(chain.sem, chain.value(row))
                    dve.tensor_tensor(s4, s4, m.unsqueeze(2).to_broadcast([P, NSLOT, NSLOT, NH]),
                                                            ALU.subtract).then_inc(signal[lane]["shifted"], 1)
                return step

            def tok_pv(lane):
                chain = chains[lane]

                def step(row):
                    dve.wait_ge(*made(lane, "ex", row))
                    p4 = pr[lane][:, :].rearrange("p (i k h) -> p i k h", i=NSLOT, k=NSLOT)
                    m = mx[lane][:, :].rearrange("p (i h) -> p i h", i=NSLOT)
                    dve.tensor_reduce(m, p4.rearrange("p i k h -> p i h k"), AX.X, ALU.add).then_inc(chain.sem, chain.tick())
                    dve.wait_ge(chain.sem, chain.value(row))
                    dve.reciprocal(mx[lane][:, :], mx[lane][:, :]).then_inc(chain.sem, chain.tick())
                    dve.wait_ge(chain.sem, chain.value(row))
                    dve.tensor_tensor(p4, p4, m.unsqueeze(2).to_broadcast([P, NSLOT, NSLOT, NH]), ALU.mult).then_inc(signal[lane]["p"], 1)
                return step

            def tok_ctx(lane):
                chain = chains[lane]

                def step(row):
                    pv = prod[lane].rearrange("p (i k f) -> p i k f", i=NSLOT, k=NSLOT)
                    c = ctxt[lane]
                    dve.wait_ge(*written(lane, "m1", row, back=1))
                    if lane == "B":
                        dve.wait_ge(*written(lane, "g1", row, back=1))
                    dve.wait_ge(*made(lane, "pvp", row))
                    dve.tensor_tensor(c[:, :, :], pv[:, :, 0, :], pv[:, :, 1, :], ALU.add).then_inc(chain.sem, chain.tick())
                    dve.wait_ge(chain.sem, chain.value(row))
                    dve.tensor_tensor(c[:, :, :], c[:, :, :], pv[:, :, 2, :], ALU.add).then_inc(signal[lane]["ctx"], 1)
                return step

            def slots(lane, fills):
                a, b = (psum(lane, f) for f in fills)
                return [a[:, 0:H], a[:, H:2 * H], b[:, 0:H]]

            def tok_ln(lane, n, fills):
                def step(row):
                    for f in fills:
                        dve.wait_ge(*written(lane, f, row))
                    statistics(lane, n, row, slots(lane, fills), EPS_TOK)
                return step

            def tok_norm(lane, n, fills, dst, after):
                def step(row):
                    dve.wait_ge(*made(lane, "rs" + n, row))
                    after(row)
                    for j, y in enumerate(slots(lane, fills)):
                        last = normalize(lane, n, j, dst[:, j, :], y)
                        if j:
                            last.then_inc(signal[lane]["z" + n], 1)
                return step

            def nothing(row):
                pass

            def next_took_zin(row):
                dve.wait_ge(*written("B", "tr1", row, back=1))

            def gate_product(row):
                for j in range(NSLOT):
                    dve.wait_ge(*made("B", "th", row, j + 1))
                    dve.scalar_tensor_tensor(out=gated[:, j, :], in0=tanh[:, j, :], scalar=1.0,
                                                             in1=psum("B", f"u{j}")[:, H:2 * H], op0=ALU.add, op1=ALU.mult).then_inc(signal["B"]["gx"], 1)
                dve.wait_ge(*made("B", "gx", row))
                for j in range(NSLOT):
                    last = dve.tensor_scalar(gated[:, j, :], gated[:, j, :],
                                             gate_mask[:, bass.ds(row.times(NSLOT, j), 1)], None, ALU.mult)
                last.then_inc(signal["B"]["gm"], 1)

            def window_sum(row):
                chain = chains["B"]
                dve.scalar_tensor_tensor(out=aux[:, :], in0=type2[:, 1, :],
                                                    scalar=kind[:, bass.ds(row.times(1, 0), 1)], in1=pos2[:, :],
                                                    op0=ALU.mult, op1=ALU.add).then_inc(chain.sem, chain.tick())
                dve.wait_ge(*written("B", "hs", row))
                dve.wait_ge(chain.sem, chain.value(row))
                dve.tensor_tensor(hpre[:, :], psum("B", "hs")[:, 0:H], aux[:, :], ALU.add).then_inc(signal["B"]["hsum"], 1)

            def norm_stats(row):
                dve.wait_ge(*made("B", "hsum", row))
                statistics("B", "3", row, [hpre[:, :]], EPS_TOK)

            def norm_out(row):
                chain = chains["B"]
                dve.wait_ge(*made("B", "rs3", row))
                normalize("B", "3", 0, hpre[:, :], hpre[:, :]).then_inc(signal["B"]["z3"], 1)
                dve.wait_ge(*made("B", "z3", row))
                dve.tensor_tensor(hpre[:, :], hpre[:, :], norm_gb[:, 0, :], ALU.mult).then_inc(signal["B"]["zg"], 1)
                dve.wait_ge(*made("B", "zg", row))
                dve.wait_ge(*made("B", "h0b", row, back=1))
                dve.tensor_tensor(h0[:, :], hpre[:, :], norm_gb[:, 1, :], ALU.add).then_inc(signal["B"]["h0"], 1)

            def c_stats(row):
                dve.wait_ge(*made("B", "h0", row))
                statistics("C", "", row, [h0[:, :]], EPS)

            def c_norm(row):
                dve.wait_ge(*made("C", "rs", row))
                dve.wait_ge(*written("C", "z", row, back=1))
                normalize("C", "", 0, c_z[:, :], h0[:, :]).then_inc(signal["C"]["z"], 1)

            def maxima(lane, fills, nm, scale):
                def step(row):
                    chain = chains[lane]
                    for f in fills:
                        dve.wait_ge(*written(lane, f"s{f}", row))
                        dve.wait_ge(*made(lane, "ex", row, f + 1, back=1))
                        cs = slice(3 * f, 3 * f + 3)
                        dve.tensor_reduce(nm[:, 0, cs], psum(lane, f"s{f}")[:, 0:384]
                                                     .rearrange("p (h t) -> p h t", h=3), AX.X, ALU.max, negate=True).then_inc(chain.sem, chain.tick())
                        dve.wait_ge(chain.sem, chain.value(row))
                        dve.tensor_scalar(nm[:, 1, cs], nm[:, 0, cs], scale, None, ALU.mult).then_inc(signal[lane]["nm"], 1)
                return step

            def inverse_sums(lane, sums):
                def step(row):
                    dve.wait_ge(*made(lane, "ex", row))
                    dve.reciprocal(sums[:, 1, :], sums[:, 0, :]).then_inc(chains[lane].sem, chains[lane].tick())
                return step

            def c_context(row):
                dve.wait_ge(chains["C"].sem, chains["C"].value(row))
                for g in range(2):
                    dve.wait_ge(*written("C", f"c{g}", row))
                    r = c_sum[:, 1, 6 * g:6 * g + 6].unsqueeze(2).to_broadcast([P, 6, AH])
                    dve.tensor_tensor(c_ctx[:, g * 384:(g + 1) * 384].rearrange("p (h e) -> p h e", h=6),
                                                       psum("C", f"c{g}")[:, 0:384].rearrange("p (h e) -> p h e", h=6),
                                                       r, ALU.mult).then_inc(signal["C"]["ctx"], 1)

            def c_out(row):
                dve.wait_ge(*written("C", "y", row))
                dve.wait_ge(*made("B", "h0b", row))
                dve.wait_ge(*made("D", "x", row, back=1))
                dve.tensor_tensor(h1[:, :], psum("C", "y")[:, 0:H], h0b[:, :], ALU.add).then_inc(signal["C"]["h1"], 1)

            def d_stats_x(row):
                dve.wait_ge(*made("C", "h1", row))
                statistics("D", "x", row, [h1[:, :]], EPS)

            def d_norm_x(row):
                dve.wait_ge(*made("D", "rsx", row))
                dve.tensor_copy(d_h1[:, :], h1[:, :]).then_inc(chains["D"].sem, chains["D"].tick())
                normalize("D", "x", 0, d_x[:, :], h1[:, :]).then_inc(signal["D"]["x"], 1)

            def d_stats_z(row):
                dve.wait_ge(*made("D", "x", row))
                statistics("D", "", row, [d_x[:, :]], EPS)

            def d_norm_z(row):
                dve.wait_ge(*made("D", "rs", row))
                normalize("D", "", 0, d_z[:, :], d_x[:, :]).then_inc(signal["D"]["z"], 1)

            def router_mean(row):
                chain = chains["D"]
                dve.wait_ge(*made("D", "eT", row))
                dve.tensor_reduce(gsum, d_eT[:, 1:P], AX.X, ALU.add).then_inc(chain.sem, chain.tick())
                dve.wait_ge(chain.sem, chain.value(row))
                dve.tensor_scalar(gmean, gsum, 1.0 / (P - 1), None, ALU.mult).then_inc(signal["D"]["gs"], 1)

            def router_h1(row):
                dve.wait_ge(*written("D", "h1", row))
                dve.tensor_tensor(hbias, psum("D", "h1")[:, P:P + 1], col("r_o1_b", P), ALU.add).then_inc(signal["D"]["hb"], 1)

            def router_bits(row):
                chain = chains["D"]
                dve.wait_ge(*written("D", "lg", row))
                dve.tensor_copy(logits, psum("D", "lg")[:, 0:4]).then_inc(signal["D"]["lgs"], 1)
                dve.wait_ge(*made("D", "lgs", row))
                dve.tensor_tensor(bits, logits[:, 1:4:2], logits[:, 0:4:2], ALU.is_gt).then_inc(chain.sem, chain.tick())
                dve.wait_ge(chain.sem, chain.value(row))
                dve.tensor_tensor(bits, bits, first[:, :], ALU.max).then_inc(chain.sem, chain.tick())
                dve.wait_ge(chain.sem, chain.value(row))
                dve.tensor_scalar(nbits, bits, -1.0, 1.0, ALU.mult, ALU.add).then_inc(chain.sem, chain.tick())
                dve.wait_ge(chain.sem, chain.value(row))
                dve.tensor_tensor(sel[:, 0:1], nbits[:, 0:1], nbits[:, 1:2], ALU.mult).then_inc(chain.sem, chain.tick())
                dve.tensor_tensor(sel[:, 1:2], nbits[:, 0:1], bits[:, 1:2], ALU.mult).then_inc(chain.sem, chain.tick())
                dve.tensor_tensor(sel[:, 2:3], bits[:, 0:1], nbits[:, 1:2], ALU.mult).then_inc(signal["D"]["sel"], 1)

            def d_context(row):
                dve.wait_ge(chains["D"].sem, chains["D"].value(row))
                dve.wait_ge(*written("D", "c", row))
                r = d_sum[:, 1, :].unsqueeze(2).to_broadcast([P, NH, DH])
                dve.tensor_tensor(d_ctx[:, :].rearrange("p (h e) -> p h e", h=NH),
                                                   psum("D", "c")[:, 0:H].rearrange("p (h e) -> p h e", h=NH), r, ALU.mult).then_inc(signal["D"]["ctx"], 1)

            def d_residual(row):
                dve.wait_ge(*written("D", "y", row))
                dve.wait_ge(*made("D", "sel", row))
                dve.scalar_tensor_tensor(out=d_h[:, :], in0=psum("D", "y")[:, 0:H], scalar=bits[:, 0:1],
                                                         in1=d_x[:, :], op0=ALU.mult, op1=ALU.add).then_inc(signal["D"]["hd"], 1)

            def d_stats_2(row):
                dve.wait_ge(*made("D", "hd", row))
                statistics("D", "2", row, [d_h[:, :]], EPS)

            def d_norm_2(row):
                dve.wait_ge(*made("D", "rs2", row))
                normalize("D", "2", 0, d_z[:, :], d_h[:, :]).then_inc(signal["D"]["z2"], 1)

            def d_mlp_out(row):
                dve.wait_ge(*written("D", "o", row))
                dve.tensor_tensor(d_ff[:, :], psum("D", "o")[:, 0:H], fc2_b[:, :], ALU.add).then_inc(signal["D"]["od"], 1)
                dve.wait_ge(*made("D", "od", row))
                dve.scalar_tensor_tensor(out=d_out[:, :], in0=d_ff[:, :], scalar=bits[:, 1:2],
                                                          in1=d_h[:, :], op0=ALU.mult, op1=ALU.add).then_inc(signal["D"]["out"], 1)

            def d_down_masked(row):
                dve.wait_ge(*written("D", "dn", row))
                for k in range(NSLOT):
                    last = dve.tensor_scalar(d_dn[:, k * RANK:(k + 1) * RANK],
                                             psum("D", "dn")[:, k * RANK:(k + 1) * RANK], sel[:, k:k + 1], None, ALU.mult)
                last.then_inc(signal["D"]["dn"], 1)

            def d_final(row):
                chain = chains["D"]
                dve.wait_ge(*written("D", "up", row))
                dve.tensor_tensor(d_out[:, :], psum("D", "up")[:, 0:H], d_out[:, :], ALU.add).then_inc(chain.sem, chain.tick())
                dve.wait_ge(chain.sem, chain.value(row))
                dve.wait_ge(*made("D", "stored", row, back=1))
                dve.tensor_tensor(d_fin[:, :], d_out[:, :], d_h1[:, :], ALU.add).then_inc(signal["D"]["fin"], 1)

            steps = {"chains": {lane: (chains[lane],) for lane in LAG}}
            for lane in TOK:
                steps[lane, "soft"] = tok_soft(lane)
                steps[lane, "pv"] = tok_pv(lane)
                steps[lane, "ctx"] = tok_ctx(lane)
                steps[lane, "ln1"] = tok_ln(lane, "1", ("y01", "y2"))
                steps[lane, "norm1"] = tok_norm(lane, "1", ("y01", "y2"), ctxt[lane], nothing)
                steps[lane, "ln2"] = tok_ln(lane, "2", ("o01", "o2"))
            steps["A", "norm2"] = tok_norm("A", "2", ("o01", "o2"), zin["B"], next_took_zin)
            steps["B", "norm2"] = tok_norm("B", "2", ("o01", "o2"), ctxt["B"], nothing)
            steps |= {("E", "stats"): emb_stats, ("E", "norm"): emb_norm, ("B", "u"): gate_product,
                      ("B", "hs"): window_sum, ("B", "ln3"): norm_stats, ("B", "norm3"): norm_out,
                      ("C", "ln"): c_stats, ("C", "norm"): c_norm,
                      ("C", "sA"): maxima("C", (0, 1), c_nm, ATT_SCALE), ("C", "sB"): maxima("C", (2, 3), c_nm, ATT_SCALE),
                      ("C", "p"): inverse_sums("C", c_sum), ("C", "c"): c_context, ("C", "y"): c_out,
                      ("D", "ln_x"): d_stats_x, ("D", "norm_x"): d_norm_x, ("D", "ln_z"): d_stats_z,
                      ("D", "norm_z"): d_norm_z, ("D", "e"): router_mean, ("D", "h1"): router_h1,
                      ("D", "lg"): router_bits,
                      ("D", "sA"): maxima("D", (0, 1), d_nm, TOK_SCALE), ("D", "sB"): maxima("D", (2, 3), d_nm, TOK_SCALE),
                      ("D", "p"): inverse_sums("D", d_sum), ("D", "c"): d_context, ("D", "y"): d_residual,
                      ("D", "ln2"): d_stats_2, ("D", "norm2"): d_norm_2, ("D", "o"): d_mlp_out,
                      ("D", "dn"): d_down_masked, ("D", "up"): d_final}
            run(dve, steps)


COLS = [("emb_g", 2), ("emb_b", 2)] + [(f"{n}{l}", 2) for l in range(2) for n in ("ln1_g", "ln1_b", "ln2_g", "ln2_b")] \
    + [("r_g", 2), ("r_b", 2), ("a_g", 2), ("a_b", 2), ("f_g", 2), ("f_b", 2)] \
    + [("r_in_b", 1), ("r_o1_b", 1), ("r_o2_b", 1)] + [(f"b1{l}", NFC) for l in range(2)] + [("fc1_b", NFC)]


def lay_out(np, a):
    f = np.float32

    def chunks(w, bias=None):
        n = w.shape[1]
        w = w.reshape(2, HC, n).transpose(1, 0, 2)
        if bias is not None:
            w = np.concatenate([w, np.stack([np.zeros(n, f), bias])[None]], 0)
        return np.ascontiguousarray(w)

    def deep(w):
        return np.ascontiguousarray(w.reshape(-1, P, w.shape[1]).transpose(1, 0, 2))

    def rows(v):
        return np.ascontiguousarray(np.broadcast_to(v, (P,) + v.shape))

    t, at, fn = (lambda n: a["L0_tok_" + n]), (lambda n: a["L0_attn_" + n]), (lambda n: a["L0_ffn_" + n])
    eye = np.eye(H, dtype=f)
    d = {"word_emb": t("word_emb"), "ident": np.eye(P, dtype=f)}
    d["shifts"] = np.stack([np.eye(P, k=-1, dtype=f), np.eye(P, dtype=f), np.eye(P, k=1, dtype=f)], 1)
    for l in range(2):
        d[f"tok_qkv{l}"] = chunks(np.concatenate([t("Wq")[l], t("Wk")[l], t("Wv")[l]], 1),
                                  np.concatenate([t("bq")[l], t("bk")[l], t("bv")[l]]))
        d[f"tok_o{l}"] = chunks(t("Wo")[l])
        d[f"tok_res1{l}"] = np.ascontiguousarray(chunks(eye, t("bo")[l])[:, 1])
        d[f"tok_res2{l}"] = np.ascontiguousarray(chunks(eye, t("b2")[l])[:, 1])
        d[f"tok_w1{l}"] = chunks(t("W1")[l])
        d[f"tok_w2{l}"] = deep(t("W2")[l])
    d["tok_gate"] = chunks(np.concatenate([t("Wg"), eye], 1), np.concatenate([t("bg"), np.zeros(H, f)]))
    cols = np.zeros((P, 64), f)
    vectors = {"emb_g": t("emb_ln_g"), "emb_b": t("emb_ln_b"), "r_g": fn("r_ln_g"), "r_b": fn("r_ln_b"),
               "a_g": fn("ln1_g"), "a_b": fn("ln1_b"), "f_g": fn("ln2_g"), "f_b": fn("ln2_b"),
               "r_in_b": fn("r_in_b"), "r_o1_b": fn("r_o1_b"), "r_o2_b": fn("r_o2_b"), "fc1_b": fn("fc1_b")}
    for l in range(2):
        vectors |= {f"{n}{l}": t(n)[l] for n in ("ln1_g", "ln1_b", "ln2_g", "ln2_b", "b1")}
    c = 0
    for name, n in COLS:
        v = vectors[name].reshape(n, -1)
        cols[0:v.shape[1], c:c + n] = v.T
        c += n
    d["cols"] = cols
    d["pos3"] = rows(t("pos_emb3").reshape(-1))
    d["type0"] = rows(t("type_emb")[0])
    d["pos2"] = t("pos_emb2")
    d["type2"] = rows(t("type_emb2"))
    d["norm_gb"] = rows(np.stack([t("norm_g"), t("norm_b")]))
    d["proj_b"] = rows(at("proj_b"))
    d["fc2_b"] = rows(fn("fc2_b"))
    first = np.zeros((P, 2), f)
    first[0] = 1.0
    d["first"] = first
    d["att_qkv"] = chunks(np.ascontiguousarray(at("qkv_w").T), at("qkv_b"))
    d["att_proj"] = deep(np.ascontiguousarray(at("proj_w").T))

    def spread(w, b):
        ws, bs = np.zeros((H, 3, 4, 32), f), np.zeros((3, 4, 32), f)
        ws[..., 0:DH] = w.T.reshape(H, 3, 4, DH)
        bs[..., 0:DH] = b.reshape(3, 4, DH)
        return ws.reshape(H, 3 * P), bs.reshape(-1)

    (wq, bq), (wk, bk) = spread(fn("wq"), fn("bq")), spread(fn("wk"), fn("bk"))
    d["ffn_qk"] = chunks(np.concatenate([wq, wk], 1), np.concatenate([bq, bk]))
    d["ffn_v"] = chunks(np.ascontiguousarray(fn("wv").T), fn("bv"))
    d["ffn_o"] = chunks(np.ascontiguousarray(fn("wo").T), fn("bo"))
    d["ffn_fc1"] = chunks(np.ascontiguousarray(fn("fc1_w").T))
    d["ffn_fc2"] = deep(np.ascontiguousarray(fn("fc2_w").T))
    d["ffn_rin"] = chunks(np.ascontiguousarray(fn("r_in_w").T))
    d["ffn_ro1"] = deep(np.ascontiguousarray(fn("r_o1_w").T))
    d["ffn_ro2"] = np.ascontiguousarray(fn("r_o2_w").T)
    d["ffn_ro3"] = np.concatenate([fn("r_o3_w").T, fn("r_o3_b")[None]], 0)
    d["ffn_down"] = chunks(np.ascontiguousarray(fn("lra_down").reshape(NSLOT * RANK, H).T))
    d["ffn_up"] = chunks(np.ascontiguousarray(fn("lra_up").transpose(0, 2, 1).reshape(NSLOT * RANK, H)))
    x = a["x"]
    win = np.zeros((P, ROWS, NSLOT), x.dtype)
    win[1:, :, 0] = x.T[:-1]
    win[:, :, 1] = x.T
    win[:-1, :, 2] = x.T[1:]
    d["ids"] = win.reshape(P, ROWS * NSLOT)
    d["kinds"] = np.ascontiguousarray(a["mask_BS_i0_1"].T)
    return d


def kernel(**inputs):
    import numpy as np
    import concourse.bacc as bacc
    from concourse.bass_utils import run_bass_kernel_spmd

    nc = bacc.Bacc("TRN2", target_bir_lowering=False, num_devices=1)
    arrays = {f"in_{k}": np.ascontiguousarray(v) for k, v in lay_out(np, {k: np.asarray(v) for k, v in inputs.items()}).items()}
    d = {k[3:]: nc.dram_tensor(k, v.shape, mybir.dt.from_np(v.dtype), kind="ExternalInput").ap()
         for k, v in arrays.items()}
    out = nc.dram_tensor("out_dram", (ROWS * P, H), F32, kind="ExternalOutput").ap()
    build_tower(nc, d, out)
    r = run_bass_kernel_spmd(nc, [arrays], core_ids=[0])
    return r.results[0]["out_dram"].reshape(ROWS, P, H)
```

```python
from contextlib import ExitStack

import concourse.bass as bass
from concourse import mybir

F32 = mybir.dt.float32
F32R = mybir.dt.float32r
I32 = mybir.dt.int32
ALU = mybir.AluOpType
ACT = mybir.ActivationFunctionType
AX = mybir.AxisListType

P = 128
H = 192
HC = H // 2
NSLOT = 3
NH = 12
DH = H // NH
FF = 768
NFC = FF // P
AH = 64
AD = NH * AH
ROWS = 64
BIG = 10000.0
EPS_TOK = 1e-12
EPS = 1e-5
TOK_SCALE = DH ** -0.5
ATT_SCALE = AH ** -0.5
RHD = 128
RANK = 64

LAG = {"E": 0, "A": 1, "B": 2, "C": 3, "D": 4}
PEEL = 5

TOK_FILLS = [("tr0", "xT", 1), ("tr1", "xT", 2),
             ("qk0", "qk", 1), ("qk1", "qk", 2), ("qk2", "qk", 3), ("v01", "v", 1), ("v2", "v", 2),
             ("c0", "cT", 1), ("c1", "cT", 2), ("y01", "ya", 1), ("y2", "ya", 2),
             ("m0", "x1T", 1), ("m1", "x1T", 2),
             ("f0", "fT", 1), ("f1", "fT", 2), ("f2", "fT", 3), ("f3", "fT", 4), ("f4", "fT", 5),
             ("f5", "fT", 6), ("o01", "oa", 1), ("o2", "oa", 2)]
FILLS = {
    "A": TOK_FILLS,
    "B": TOK_FILLS + [("g0", "gT", 1), ("g1", "gT", 2), ("u01", "th", 1), ("u2", "th", 2),
                      ("hs", "hsum", 1)],
    "C": [("z", "zT", 1), ("qk0", "qkT", 1), ("qk1", "qkT", 2), ("qk2", "qkT", 3), ("v0", "v", 1),
          ("v1", "v", 2), ("s0", "ex", 1), ("s1", "ex", 2), ("s2", "ex", 3), ("s3", "ex", 4),
          ("p0", "pT", 1), ("p1", "pT", 2), ("p2", "pT", 3), ("c0", "cT", 1), ("c1", "cT", 2),
          ("y", "h1", 1)],
    "D": [("z", "zT", 1), ("qk0", "qkT", 1), ("qk1", "qkT", 2), ("v", "v", 1), ("e", "eT", 1),
          ("s0", "ex", 1), ("s1", "ex", 2), ("s2", "ex", 3), ("s3", "ex", 4),
          ("h1", "h1T", 1), ("h2", "h2T", 1),
          ("p0", "pT", 1), ("p1", "pT", 2), ("p2", "pT", 3), ("lg", "lgs", 1), ("c", "ctx", 1),
          ("t", "cT", 1), ("y", "hd", 1), ("z2", "z2T", 1), ("f0", "fT", 1), ("f1", "fT", 2),
          ("o", "od", 1), ("ot", "oT", 1), ("dn", "dn", 1), ("dt", "dT", 1), ("up", "fin", 1)],
}
BANK0 = {"A": 0, "B": 2, "C": 4, "D": 6}

TOK_SIGNALS = dict(xT=2, qk=3, v=2, qkp=3, shifted=1, ex=1, p=1, pvp=3, ctx=1, cT=2,
                   ya=2, ve1=1, rs1=1, z1=1, x1T=2, x1lo=2, fT=6, oa=2, ve2=1, rs2=1, z2=1,
                   rg=1, res=1, rg1=1, res1=1)
SIGNALS = {
    "E": dict(idx=1, loaded=48, emb=1, ve=1, rs=1),
    "A": TOK_SIGNALS | dict(zin=1),
    "B": TOK_SIGNALS | dict(rgg=1, resg=1, gT=2, th=2, gx=1, gm=1, hsum=1, ve3=1, rs3=1, z3=1, zg=1, h0=1,
                            h0b=1),
    "C": dict(ve=1, rs=1, z=1, zT=1, qkT=3, v=2, nm=4, ex=4, pn=3, pT=3, cT=2, h1=1),
    "D": dict(vex=1, rsx=1, x=1, ve=1, rs=1, z=1, zT=1, zrT=1, eT=1, gs=1, hb=1, h1T=1, h2T=1,
              lgs=1, sel=1, qkT=2, v=1, nm=4, ex=4, pT=3, ctx=1, cT=1, hd=1, ve2=1, rs2=1, z2=1,
              z2T=1, fT=2, od=1, out=1, oT=1, dn=1, dT=1, fin=1, stored=16),
}
C_HEADS = [[0, 2, 4], [1, 3, 5], [6, 8, 10], [7, 9, 11]]
D_HEADS = [[r, r + 4, r + 8] for r in range(4)]

ORDER = [
    ("B", "tr"), ("B", "res"), ("D", "ln_x"), ("A", "tr"), ("C", "ln"), ("D", "norm_x"), ("B", "qkv"),
    ("C", "norm"), ("C", "z"), ("A", "res"), ("B", "qkp"), ("D", "ln_z"), ("A", "qkv"), ("A", "qkp"),
    ("B", "soft"), ("C", "qk"), ("D", "norm_z"), ("B", "pv"), ("A", "soft"), ("C", "v"), ("A", "pv"),
    ("C", "sA"), ("B", "ctx"), ("A", "ctx"), ("D", "qk"), ("D", "e"), ("B", "tc"), ("A", "tc"),
    ("D", "sA"), ("C", "sB"), ("B", "y"), ("D", "sB"), ("A", "y"), ("E", "gather"), ("B", "ln1"),
    ("D", "h1"), ("C", "p"), ("B", "norm1"), ("A", "ln1"), ("D", "h2"), ("D", "p"), ("D", "lg"),
    ("B", "res1"), ("B", "m"), ("A", "norm1"), ("C", "c"), ("D", "c"), ("B", "ff"), ("A", "res1"),
    ("E", "stats"), ("A", "m"), ("B", "o"), ("B", "ln2"), ("D", "t"), ("A", "ff"), ("B", "norm2"),
    ("D", "y"), ("D", "ln2"), ("D", "norm2"), ("B", "resg"), ("C", "y"), ("B", "g"), ("D", "z2"),
    ("A", "o"), ("A", "ln2"), ("D", "ff"), ("A", "norm2"), ("B", "u"), ("D", "o"), ("E", "norm"),
    ("D", "ot"), ("B", "hs"), ("D", "dn"), ("D", "dt"), ("B", "ln3"), ("B", "norm3"), ("B", "h0"),
    ("D", "up"),
]


class Row:

    def __init__(self, turn, base, lag):
        self.turn, self.base = turn, base - lag

    def times(self, k, c):
        c += k * self.base
        if self.turn is None:
            return c
        return self.turn * k + c if c else self.turn * k


class Chain:

    def __init__(self, sem):
        self.sem, self.count, self.per_row = sem, 0, 0

    def begin(self, row):
        if self.count:
            self.per_row = self.count
        self.count = 0

    def tick(self):
        self.count += 1
        return 1

    def value(self, row):
        return row.times(self.per_row, self.count)


def build_tower(nc, d, out):
    with ExitStack() as ctx:
        def sb(name, shape, dt=F32):
            return ctx.enter_context(nc.sbuf_tensor(name, shape, dt))

        def sem(name):
            return ctx.enter_context(nc.semaphore(name))

        bank = [ctx.enter_context(nc.psum_tensor(f"bank{i}", [P, 512], F32)) for i in range(8)]
        full = [sem(f"full{i}") for i in range(8)]
        signal = {lane: {name: sem(f"{lane}_{name}") for name in SIGNALS[lane]} for lane in SIGNALS}
        weights_loaded = sem("weights_loaded")
        late_weights_loaded = sem("late_weights_loaded")
        masks_ready = sem("masks_ready")
        const_ready = sem("const_ready")

        loads = []

        def weight(name, shape, dt=F32):
            t = sb("w_" + name, shape, dt)
            loads.append((t, name))
            return t

        ident = weight("ident", [P, P])
        shifts = weight("shifts", [P, NSLOT, P])
        wqkv = [weight(f"tok_qkv{l}", [HC + 1, 2, 3 * H]) for l in range(2)]
        wo = [weight(f"tok_o{l}", [HC, 2, H]) for l in range(2)]
        gains = weight("gains", [P, 5, H])
        shift = weight("norm_shift", [P, 5, H])
        w2 = [weight(f"tok_w2{l}", [P, NFC, H]) for l in range(2)]
        wgate = weight("tok_gate", [HC + 1, 2, H])
        cols = weight("cols", [P, 64])
        pos3 = weight("pos3", [P, NSLOT * H])
        pos2 = weight("pos2", [P, H])
        type2 = weight("type2", [P, 2, H])
        norm_gb = weight("norm_gb", [P, 2, H])
        proj_b = weight("proj_b", [P, H])
        fc2_b = weight("fc2_b", [P, H])
        first = weight("first", [P, 2])
        early = len(loads)
        c_qkv = weight("att_qkv", [HC + 1, 2, 3 * AD])
        c_proj = weight("att_proj", [P, AD // P, H])
        d_qk = weight("ffn_qk", [HC + 1, 2, 6 * P])
        d_v = weight("ffn_v", [HC + 1, 2, H])
        d_o = weight("ffn_o", [HC + 1, 2, H])
        d_fc1 = weight("ffn_fc1", [HC, 2, FF])
        d_fc2 = weight("ffn_fc2", [P, NFC, H])
        d_rin = weight("ffn_rin", [HC, 2, RHD])
        d_ro1 = weight("ffn_ro1", [RHD, 2, RHD])
        d_ro2 = weight("ffn_ro2", [RHD, RHD // 2])
        d_ro3 = weight("ffn_ro3", [RHD // 2 + 1, 4])
        d_down = weight("ffn_down", [HC, 2, NSLOT * RANK])
        d_up = weight("ffn_up", [HC, 2, H])
        early_loads, late_loads = loads[:early], loads[early:]
        loads = early_loads
        ids = weight("ids", [P, ROWS * NSLOT], I32)
        kinds = weight("kinds", [P, ROWS], I32)
        col_at = {}
        at = 0
        for name, n in COLS:
            col_at[name] = at
            at += n
        assert at <= 64

        def col(name, parts, k=0):
            c = col_at[name] + k
            return cols[0:parts, c:c + 1]

        mask = sb("mask", [P, ROWS * NSLOT])
        gate_mask = sb("gate_mask", [P, ROWS * NSLOT])
        att_bias = mask
        kind = sb("kind", [P, ROWS])
        scratch = sb("scratch", [P, 2])
        minus_half = sb("minus_half", [P, NSLOT])

        idx = sb("idx", [P, 4], I32)
        emb = sb("emb", [P, NSLOT, H])

        TOK = "AB"
        xT = {l: sb(f"{l}_xT", [HC + 1, 2, NSLOT * P]) for l in TOK}
        qkv = {l: sb(f"{l}_qkv", [P, NSLOT, 3 * H]) for l in TOK}
        fT = {l: sb(f"{l}_fT", [P, NFC, NSLOT * P]) for l in TOK}
        flat = {l: fT[l][:, :, :].rearrange("p a b -> p (a b)") for l in TOK}
        prod = {l: flat[l][:, 0:9 * H] for l in TOK}
        xres = {l: flat[l][:, 9 * H:12 * H].rearrange("p (j f) -> p j f", j=NSLOT) for l in TOK}
        x1res = {l: qkv[l][:, :, 0:H] for l in TOK}
        z1_twice = {l: qkv[l][:, :, H:H + P] for l in TOK}
        cT = {l: fT[l][0:HC, 0:2, :] for l in TOK}
        ctxt = {l: sb(f"{l}_ctx", [P, NSLOT, H]) for l in TOK}
        zin = {"A": emb, "B": ctxt["A"]}
        x1f = sb("x1f", [P, 2, NSLOT * P])
        x1_high = sb("x1_high", [P, NSLOT * P], F32R)
        x1_low = sb("x1_low", [P, NSLOT * P], F32R)
        x1_both = sb("x1_both", [P, NSLOT * P], F32R)
        high_rows = [slice(0, H - P), slice(H - P, P)]
        low_rows = [high_rows[1], high_rows[0]]
        w1_high = [sb(f"w1_high{l}", [P, FF], F32R) for l in range(2)]
        w1_low = [sb(f"w1_low{l}", [P, FF], F32R) for l in range(2)]
        w1_both = [sb(f"w1_both{l}", [P, FF], F32R) for l in range(2)]
        w1_rest = sb("w1_rest", [P, FF], F32R)
        w1_raw = {l: flat[l][:, 0:2 * FF].rearrange("p (c f) -> p c f", c=2) for l in TOK}
        out_bias = flat["A"][:, 2 * FF:2 * FF + 4 * H].rearrange("p (k f) -> p k f", k=4)
        type0 = flat["B"][:, 2 * FF:2 * FF + H]
        loads += [(w1_raw["A"], "tok_w10"), (w1_raw["B"], "tok_w11"), (out_bias, "out_bias"), (type0, "type0")]
        sc = {l: sb(f"{l}_sc", [P, NSLOT * NSLOT * NH]) for l in TOK}
        pr = {l: sb(f"{l}_pr", [P, NSLOT * NSLOT * NH]) for l in TOK}
        mx = {l: sb(f"{l}_mx", [P, NSLOT * NH]) for l in TOK}
        gated = qkv["B"][:, :, 0:H]
        tanh = qkv["B"][:, :, H:2 * H]
        xgate = qkv["B"][:, :, 2 * H:3 * H]
        hpre = sb("hpre", [P, H])
        h0 = sb("h0", [P, H])
        h0b = sb("h0b", [P, H])

        LNS = [("E", "", 3), ("A", "1", 3), ("A", "2", 3), ("B", "1", 3), ("B", "2", 3), ("B", "3", 1),
               ("C", "", 1), ("D", "x", 1), ("D", "", 1), ("D", "2", 1)]
        lnst = {(l, n): (sb(f"{l}_st{n}", [P, k, 6]), sb(f"{l}_mv{n}", [P, k, 2]),
                         sb(f"{l}_ve{n}_", [P, k]), sb(f"{l}_rs{n}_", [P, k])) for l, n, k in LNS}

        c_z = sb("C_z", [P, H])
        c_zT = sb("C_zT", [HC + 1, 2, P])
        c_qkT = sb("C_qkT", [P, NH, P])
        c_v = sb("C_v", [P, AD])
        c_p = sb("C_p", [P, NH, P])
        c_cT = c_p[:, 6:12, :]
        c_nm = sb("C_nm", [P, 2, 12])
        c_sum = sb("C_sum", [P, 2, NH])
        h1 = sb("h1", [P, H])

        d_x = sb("D_x", [P, H])
        d_h1 = sb("D_h1", [P, H])
        d_z = sb("D_z", [P, H])
        d_zT = sb("D_zT", [HC + 1, 2, P])
        d_zrT = sb("D_zrT", [HC, 2, P])
        d_eT = sb("D_eT", [P, P])
        d_h1T = sb("D_h1T", [P, P])
        d_h2T = sb("D_h2T", [RHD // 2 + 1, P])
        d_small = sb("D_small", [P, 32])
        d_pT = sb("D_pT", [P, NH, P])
        d_qkT = d_pT[:, 0:6, :]
        d_vs = sb("D_v", [P, H])
        d_p = sb("D_p", [P, NH, P])
        d_fT = d_p[:, 0:NFC, :]
        d_nm = sb("D_nm", [P, 2, 12])
        d_sum = sb("D_sum", [P, 2, NH])
        d_ctx = sb("D_ctx", [P, H])
        d_cT = d_zT
        d_h = sb("D_h", [P, H])
        d_z2T = d_zrT
        d_ff = d_ctx
        d_out = sb("D_out", [P, H])
        d_oT = d_zrT
        d_dn = d_z

        bits = d_small[:, 0:2]
        nbits = d_small[:, 2:4]
        sel = d_small[:, 4:7]
        logits = d_small[:, 8:12]
        gsum = d_small[:, 12:13]
        hbias = d_small[:, 13:14]
        gmean = d_small[:, 14:15]

        place, on_bank = {}, {b: 0 for b in range(8)}
        before = {}
        claims = dict.fromkeys(FILLS, 0)
        for lane, fills in FILLS.items():
            last = [None, None]
            for n, (fill, name, value) in enumerate(fills):
                b = BANK0[lane] + n % 2
                on_bank[b] += 1
                place[lane, fill] = (b, on_bank[b])
                before[lane, fill] = last[n % 2]
                last[n % 2] = (name, value, 0)
            for fill, *_ in fills[:2]:
                k = place[lane, fill][0] - BANK0[lane]
                before[lane, fill] = (*last[k][:2], 1)

        def made(lane, name, row, value=None, back=0):
            per = SIGNALS[lane][name]
            n = row.times(per, (per if value is None else value) - back * per)
            return reached(signal[lane][name], n)

        def written(lane, fill, row, back=0):
            b, k = place[lane, fill]
            return reached(full[b], row.times(on_bank[b], k - back * on_bank[b]))

        def drained(lane, fill, row):
            assert fill == FILLS[lane][claims[lane] % len(FILLS[lane])][0]
            claims[lane] += 1
            name, value, back = before[lane, fill]
            return made(lane, name, row, value, back)

        def reached(sem, n):
            return (const_ready, 3) if isinstance(n, int) and n <= 0 else (sem, n)

        def bank_of(lane, fill):
            return place[lane, fill][0]

        def psum(lane, fill):
            return bank[place[lane, fill][0]]

        def run(engine, steps):
            def turn(reg, base, lanes):
                rows = {lane: Row(reg, base, LAG[lane]) for lane in LAG}
                for lane in lanes:
                    for chain in steps.get("chains", {}).get(lane, ()):
                        chain.begin(rows[lane])
                for lane, step in ORDER:
                    if lane in lanes and (lane, step) in steps:
                        steps[lane, step](rows[lane])
            for t in range(PEEL):
                turn(None, t, [l for l in LAG if t >= LAG[l]])
            with engine.Fori(0, ROWS - PEEL) as reg:
                turn(reg, PEEL, list(LAG))
            for t in range(ROWS, ROWS + LAG["D"]):
                turn(None, t, [l for l in LAG if t < ROWS + LAG[l]])

        block = ctx.enter_context(nc.Block())

        @block.sync
        def _(sp):
            for t, name in loads:
                sp.dma_start(t[tuple(slice(None) for _ in t.shape)], d[name]).then_inc(weights_loaded, 16)

            for t, name in late_loads:
                sp.dma_start(t[tuple(slice(None) for _ in t.shape)], d[name]).then_inc(late_weights_loaded, 16)

            def store(row):
                sp.wait_ge(*made("D", "fin", row))
                sp.dma_start(out[bass.ds(row.times(P, 0), P), :], d_out[:, :]).then_inc(signal["D"]["stored"], 16)
            run(sp, {("D", "up"): store})
            sp.wait_ge(signal["D"]["stored"], 16 * ROWS)

        @block.gpsimd
        def _(pool):
            pool.memset(minus_half[:, :], -0.5).then_inc(const_ready, 1)
            pool.wait_ge(weights_loaded, 16 * len(loads))
            pool.wait_ge(const_ready, 2)
            for j in range(NSLOT):
                last = pool.tensor_tensor(pos3[:, j * H:(j + 1) * H], pos3[:, j * H:(j + 1) * H],
                                          type0, ALU.add)
            last.then_inc(const_ready, 1)
            pool.wait_ge(const_ready, 3)

            def gather(row):
                pool.wait_ge(*made("E", "loaded", row, back=1))
                pool.tensor_copy(idx[:, 0:NSLOT], ids[:, bass.ds(row.times(NSLOT, 0), NSLOT)]
                                 ).then_inc(signal["E"]["idx"], 1)
                pool.wait_ge(*made("E", "idx", row))
                pool.wait_ge(*made("A", "rg", row, back=1))
                pool.wait_ge(*written("A", "tr1", row, back=1))
                pool.tensor_tensor(scratch[:, 1:2], minus_half[:, 0:1], minus_half[:, 0:1], ALU.add)
                for j in range(NSLOT):
                    pool.indirect_dma_start(emb[:, j, :], None, d["word_emb"],
                                            bass.IndirectOffsetOnAxis(idx[:, j:j + 1], 0)
                                            ).then_inc(signal["E"]["loaded"], 16)

            def add_positions(row):
                pool.wait_ge(*made("E", "loaded", row))
                pool.tensor_tensor(emb[:, :, :], emb[:, :, :], pos3[:, :].rearrange("p (j f) -> p j f", j=NSLOT), ALU.add
                                   ).then_inc(signal["E"]["emb"], 1)

            def inverse_deviation(lane, n=""):
                def step(row):
                    pool.wait_ge(*made(lane, "ve" + n, row))
                    _, _, ve, rs = lnst[lane, n]
                    pool.tensor_tensor(rs[:, :], ve[:, :], minus_half[:, 0:ve.shape[1]], ALU.pow
                                       ).then_inc(signal[lane]["rs" + n], 1)
                return step

            def qk_products(lane):
                def step(row):
                    pool.wait_ge(*made(lane, "qk", row))
                    pool.wait_ge(*written(lane, "o2", row, back=1))
                    pv = prod[lane].rearrange("p (i k f) -> p i k f", i=NSLOT, k=NSLOT)
                    for i in range(NSLOT):
                        q = qkv[lane][:, i, 0:H].unsqueeze(1).to_broadcast([P, NSLOT, H])
                        pool.tensor_tensor(pv[:, i, :, :], q, qkv[lane][:, :, H:2 * H], ALU.mult
                                           ).then_inc(signal[lane]["qkp"], 1)
                return step

            def pv_products(lane):
                def step(row):
                    pool.wait_ge(*made(lane, "p", row))
                    pool.wait_ge(*made(lane, "v", row))
                    pv = prod[lane].rearrange("p (i k h d) -> p i k h d", i=NSLOT, k=NSLOT, h=NH)
                    pp = pr[lane][:, :].rearrange("p (i k h) -> p i k h", i=NSLOT, k=NSLOT)
                    for i in range(NSLOT):
                        for k in range(NSLOT):
                            v = qkv[lane][:, k, 2 * H:3 * H].rearrange("p (h d) -> p h d", h=NH)
                            w = pp[:, i, k, :].unsqueeze(2).to_broadcast([P, NH, DH])
                            last = pool.tensor_tensor(pv[:, i, k], v, w, ALU.mult)
                        last.then_inc(signal[lane]["pvp"], 1)
                return step

            def affine(lane, k, src, dst, z, scaled, result):
                def step(row):
                    pool.wait_ge(*made(*z, row))
                    if result != "res1":
                        pool.wait_ge(*written(lane, "hs" if result == "resg" else "o2", row, back=1))
                    g = gains[:, k, :].unsqueeze(1).to_broadcast([P, NSLOT, H])
                    b = shift[:, k, :].unsqueeze(1).to_broadcast([P, NSLOT, H])
                    pool.tensor_tensor(dst, src[:, :, :], g, ALU.mult).then_inc(signal[lane][scaled], 1)
                    pool.wait_ge(*made(lane, scaled, row))
                    pool.tensor_tensor(dst, dst, b, ALU.add).then_inc(signal[lane][result], 1)
                return step

            def add_proj_bias(row):
                pool.wait_ge(*made("B", "h0", row))
                pool.wait_ge(*made("C", "h1", row, back=1))
                pool.tensor_tensor(h0b[:, :], h0[:, :], proj_b[:, :], ALU.add
                                   ).then_inc(signal["B"]["h0b"], 1)

            steps = {("E", "gather"): gather, ("E", "stats"): add_positions, ("E", "norm"): inverse_deviation("E"),
                     ("B", "h0"): add_proj_bias}
            for n, l in enumerate(TOK):
                steps[l, "res"] = affine(l, 2 * n, zin[l], xres[l], ("A", "zin" if n == 0 else "z2"), "rg", "res")
                steps[l, "res1"] = affine(l, 2 * n + 1, ctxt[l], x1res[l], (l, "z1"), "rg1", "res1")
                steps[l, "qkp"] = qk_products(l)
                steps[l, "pv"] = pv_products(l)
                steps[l, "ln1"] = inverse_deviation(l, "1")
                steps[l, "ln2"] = inverse_deviation(l, "2")
            steps["B", "resg"] = affine("B", 4, ctxt["B"], xgate, ("B", "z2"), "rgg", "resg")
            steps["B", "ln3"] = inverse_deviation("B", "3")
            steps["C", "ln"] = inverse_deviation("C")
            steps["D", "ln_x"] = inverse_deviation("D", "x")
            steps["D", "ln_z"] = inverse_deviation("D")
            steps["D", "ln2"] = inverse_deviation("D", "2")
            run(pool, steps)

        @block.tensor
        def _(pe):
            pe.wait_ge(weights_loaded, 16 * len(loads))
            pe.wait_ge(const_ready, 3)

            def transpose_slots(lane, row, src, fills):
                for c, fill in enumerate(fills):
                    pe.wait_ge(*drained(lane, fill, row))
                    dst = psum(lane, fill)
                    for j in range(NSLOT):
                        last = pe.transpose(dst[0:HC, j * P:(j + 1) * P], src[:, j, c * HC:(c + 1) * HC], ident[:, :])
                    last.then_inc(full[bank_of(lane, fill)], 1)

            def transpose_pair(lane, row, src, fill):
                pe.wait_ge(*drained(lane, fill, row))
                dst = psum(lane, fill)
                for c in range(2):
                    last = pe.transpose(dst[0:HC, c * P:(c + 1) * P], src[:, c * HC:(c + 1) * HC], ident[:, :])
                last.then_inc(full[bank_of(lane, fill)], 1)

            def tok_tr(lane):
                def step(row):
                    pe.wait_ge(*made("A", "zin" if lane == "A" else "z2", row))
                    transpose_slots(lane, row, zin[lane], ("tr0", "tr1"))
                return step

            def tok_qkv(lane, l):
                def step(row):
                    pe.wait_ge(*made(lane, "xT", row))
                    w = wqkv[l]
                    x = xT[lane]
                    for j in range(NSLOT):
                        pe.wait_ge(*drained(lane, f"qk{j}", row))
                        dst = psum(lane, f"qk{j}")
                        tok = slice(j * P, (j + 1) * P)
                        pe.matmul(dst[:, 0:2 * H], x[0:HC, 0, tok], w[0:HC, 0, 0:2 * H], start=True, stop=False)
                        pe.matmul(dst[:, 0:2 * H], x[:, 1, tok], w[:, 1, 0:2 * H],
                                                        start=False, stop=True).then_inc(full[bank_of(lane, f"qk{j}")], 1)
                    for fill, slots in (("v01", (0, 1)), ("v2", (2,))):
                        pe.wait_ge(*drained(lane, fill, row))
                        dst = psum(lane, fill)
                        for n, j in enumerate(slots):
                            tok = slice(j * P, (j + 1) * P)
                            o = dst[:, n * H:(n + 1) * H]
                            pe.matmul(o, x[0:HC, 0, tok], w[0:HC, 0, 2 * H:], start=True, stop=False)
                            last = pe.matmul(o, x[:, 1, tok], w[:, 1, 2 * H:], start=False, stop=True)
                        last.then_inc(full[bank_of(lane, fill)], 1)
                return step

            def tok_tc(lane):
                def step(row):
                    pe.wait_ge(*made(lane, "ctx", row))
                    transpose_slots(lane, row, ctxt[lane], ("c0", "c1"))
                return step

            def tok_y(lane, l):
                def step(row):
                    pe.wait_ge(*made(lane, "cT", row))
                    for fill, slots in (("y01", (0, 1)), ("y2", (2,))):
                        pe.wait_ge(*drained(lane, fill, row))
                        dst = psum(lane, fill)
                        for n, j in enumerate(slots):
                            tok = slice(j * P, (j + 1) * P)
                            o = dst[:, n * H:(n + 1) * H]
                            pe.matmul(o, cT[lane][0:HC, 0, tok], wo[l][:, 0, :], start=True, stop=False)
                            last = pe.matmul(o, cT[lane][0:HC, 1, tok], wo[l][:, 1, :], start=False, stop=True)
                        last.then_inc(full[bank_of(lane, fill)], 1)
                return step

            def tok_m(lane):
                def step(row):
                    pe.wait_ge(*made(lane, "z1", row))
                    for fill in ("m0", "m1"):
                        pe.wait_ge(*drained(lane, fill, row))
                        dst = psum(lane, fill)
                        for j in range(NSLOT):
                            z = ctxt[lane][:, j, 0:P] if fill == "m0" else z1_twice[lane][:, j, :]
                            last = pe.transpose(dst[:, j * P:(j + 1) * P], z, ident[:, :])
                        last.then_inc(full[bank_of(lane, fill)], 1)
                return step

            def tok_ff(lane, l):
                high = high_rows[l]

                def step(row):
                    pe.wait_ge(*made(lane, "x1lo", row))
                    for f in range(NFC):
                        fill = f"f{f}"
                        pe.wait_ge(*drained(lane, fill, row))
                        o = psum(lane, fill)[:, 0:NSLOT * P]
                        fs = slice(f * P, (f + 1) * P)
                        pe.matmul(o, w1_high[l][:, fs], x1_high[:, :], start=True, stop=False)
                        pe.matmul(o, w1_high[l][:, fs], x1_low[:, :], start=False, stop=False)
                        pe.matmul(o, w1_low[l][:, fs], x1_high[:, :], start=False, stop=False)
                        pe.matmul(o, w1_both[l][:, fs], x1_both[:, :], start=False, stop=False)
                        pe.matmul(o, w1_rest[high, fs], x1_both[high, :], start=False, stop=True
                                  ).then_inc(full[bank_of(lane, fill)], 1)
                return step

            def tok_o(lane, l):
                def step(row):
                    pe.wait_ge(*made(lane, "fT", row))
                    for fill, slots in (("o01", (0, 1)), ("o2", (2,))):
                        pe.wait_ge(*drained(lane, fill, row))
                        dst = psum(lane, fill)
                        for n, j in enumerate(slots):
                            tok = slice(j * P, (j + 1) * P)
                            o = dst[:, n * H:(n + 1) * H]
                            for f in range(NFC):
                                last = pe.matmul(o, fT[lane][:, f, tok], w2[l][:, f, :], start=(f == 0),
                                                 stop=(f == NFC - 1))
                        last.then_inc(full[bank_of(lane, fill)], 1)
                return step

            def gate_tr(row):
                pe.wait_ge(*made("B", "z2", row))
                transpose_slots("B", row, ctxt["B"], ("g0", "g1"))

            def gate(row):
                pe.wait_ge(*made("B", "gT", row))
                for fill, slots in (("u01", (0, 1)), ("u2", (2,))):
                    pe.wait_ge(*drained("B", fill, row))
                    dst = psum("B", fill)
                    for n, j in enumerate(slots):
                        tok = slice(j * P, (j + 1) * P)
                        o = dst[:, n * H:(n + 1) * H]
                        pe.matmul(o, xT["B"][0:HC, 0, tok], wgate[0:HC, 0, :], start=True, stop=False)
                        last = pe.matmul(o, xT["B"][:, 1, tok], wgate[:, 1, :], start=False, stop=True)
                    last.then_inc(full[bank_of("B", fill)], 1)

            def window_sum(row):
                pe.wait_ge(*made("B", "gm", row))
                pe.wait_ge(*drained("B", "hs", row))
                dst = psum("B", "hs")
                for n, j in enumerate((1, 0, 2)):
                    last = pe.matmul(dst[:, 0:H], shifts[:, j, :], gated[:, j, :], start=(n == 0), stop=(n == 2))
                last.then_inc(full[bank_of("B", "hs")], 1)

            def c_z_tr(row):
                if row.turn is None:
                    pe.wait_ge(late_weights_loaded, 16 * len(late_loads))
                pe.wait_ge(*made("C", "z", row))
                transpose_pair("C", row, c_z, "z")

            def c_qk(row):
                pe.wait_ge(*made("C", "zT", row))
                for g in range(3):
                    pe.wait_ge(*drained("C", f"qk{g}", row))
                    dst = psum("C", f"qk{g}")
                    for k in range(4):
                        m = 4 * g + k
                        o = dst[:, k * P:(k + 1) * P]
                        ws = slice(m * P, (m + 1) * P)
                        pe.matmul(o, c_qkv[0:HC, 0, ws], c_zT[0:HC, 0, :], start=True, stop=False)
                        last = pe.matmul(o, c_qkv[:, 1, ws], c_zT[:, 1, :], start=False, stop=True)
                    last.then_inc(full[bank_of("C", f"qk{g}")], 1)

            def c_values(row):
                for g in range(2):
                    pe.wait_ge(*drained("C", f"v{g}", row))
                    dst = psum("C", f"v{g}")
                    ws = slice(2 * AD + g * 384, 2 * AD + (g + 1) * 384)
                    pe.matmul(dst[:, 0:384], c_zT[0:HC, 0, :], c_qkv[0:HC, 0, ws], start=True, stop=False)
                    pe.matmul(dst[:, 0:384], c_zT[:, 1, :], c_qkv[:, 1, ws],
                                                  start=False, stop=True).then_inc(full[bank_of("C", f"v{g}")], 1)

            def c_scores(fills):
                def step(row):
                    pe.wait_ge(*made("C", "qkT", row))
                    for f in fills:
                        pe.wait_ge(*drained("C", f"s{f}", row))
                        dst = psum("C", f"s{f}")
                        for n, h in enumerate(C_HEADS[f]):
                            r = slice(AH * (h % 2), AH * (h % 2) + AH)
                            last = pe.matmul(dst[:, n * P:(n + 1) * P], c_qkT[r, h // 2, :], c_qkT[r, 6 + h // 2, :],
                                             start=True, stop=True)
                        last.then_inc(full[bank_of("C", f"s{f}")], 1)
                return step

            def transpose_p(lane, probs):
                def step(row):
                    if lane == "D":
                        pe.wait_ge(*made(lane, "ex", row))
                    for g in range(3):
                        if lane == "C":
                            pe.wait_ge(*made(lane, "pn", row, g + 1))
                        pe.wait_ge(*drained(lane, f"p{g}", row))
                        dst = psum(lane, f"p{g}")
                        for k in range(4):
                            last = pe.transpose(dst[:, k * P:(k + 1) * P], probs[:, 4 * g + k, :], ident[:, :])
                        last.then_inc(full[bank_of(lane, f"p{g}")], 1)
                return step

            def c_context(row):
                pe.wait_ge(*made("C", "pT", row))
                pe.wait_ge(*made("C", "v", row))
                for g in range(2):
                    pe.wait_ge(*drained("C", f"c{g}", row))
                    dst = psum("C", f"c{g}")
                    for k in range(6):
                        h = 6 * g + k
                        r = slice(AH * (k % 2), AH * (k % 2) + AH)
                        last = pe.matmul(dst[r, k // 2 * P:(k // 2 + 1) * P], c_v[:, h * AH:(h + 1) * AH], c_qkT[:, h, :],
                                         start=True, stop=True)
                    last.then_inc(full[bank_of("C", f"c{g}")], 1)

            def c_out(row):
                pe.wait_ge(*made("C", "cT", row))
                pe.wait_ge(*drained("C", "y", row))
                dst = psum("C", "y")
                for m in range(6):
                    last = pe.matmul(dst[:, 0:H], c_cT[:, m, :], c_proj[:, m, :], start=(m == 0), stop=(m == 5))
                last.then_inc(full[bank_of("C", "y")], 1)

            def d_qkv(row):
                pe.wait_ge(*made("D", "z", row))
                transpose_pair("D", row, d_z, "z")

            def router_e(row):
                pe.wait_ge(*made("D", "zrT", row))
                pe.wait_ge(*drained("D", "e", row))
                dst = psum("D", "e")
                for c in range(2):
                    last = pe.matmul(dst[:, 0:P], d_rin[:, c, :], d_zrT[:, c, :], start=(c == 0), stop=(c == 1))
                last.then_inc(full[bank_of("D", "e")], 1)

            def router_h1(row):
                pe.wait_ge(*made("D", "gs", row))
                pe.wait_ge(*drained("D", "h1", row))
                dst = psum("D", "h1")
                pe.matmul(dst[:, 0:P], d_ro1[:, 0, :], d_eT[:, :], start=True, stop=True)
                pe.matmul(dst[:, P:P + 1], d_ro1[:, 1, :], gmean, start=True, stop=True).then_inc(full[bank_of("D", "h1")], 1)

            def router_h2(row):
                pe.wait_ge(*made("D", "h1T", row))
                pe.wait_ge(*drained("D", "h2", row))
                dst = psum("D", "h2")
                pe.matmul(dst[0:RHD // 2, 0:P], d_ro2[:, :], d_h1T[:, :], start=True, stop=True).then_inc(full[bank_of("D", "h2")], 1)

            def router_logits(row):
                pe.wait_ge(*made("D", "h2T", row))
                pe.wait_ge(*drained("D", "lg", row))
                dst = psum("D", "lg")
                pe.matmul(dst[:, 0:4], d_h2T[:, :], d_ro3[:, :], start=True, stop=True).then_inc(full[bank_of("D", "lg")], 1)

            def d_heads(row):
                pe.wait_ge(*made("D", "zT", row))
                for g in range(2):
                    pe.wait_ge(*drained("D", f"qk{g}", row))
                    dst = psum("D", f"qk{g}")
                    for k in range(3):
                        m = 3 * g + k
                        o = dst[:, k * P:(k + 1) * P]
                        ws = slice(m * P, (m + 1) * P)
                        pe.matmul(o, d_qk[0:HC, 0, ws], d_zT[0:HC, 0, :], start=True, stop=False)
                        last = pe.matmul(o, d_qk[:, 1, ws], d_zT[:, 1, :], start=False, stop=True)
                    last.then_inc(full[bank_of("D", f"qk{g}")], 1)
                pe.wait_ge(*drained("D", "v", row))
                dst = psum("D", "v")
                pe.matmul(dst[:, 0:H], d_zT[0:HC, 0, :], d_v[0:HC, 0, :], start=True, stop=False)
                pe.matmul(dst[:, 0:H], d_zT[:, 1, :], d_v[:, 1, :], start=False, stop=True).then_inc(full[bank_of("D", "v")], 1)

            def d_scores(fills):
                def step(row):
                    pe.wait_ge(*made("D", "qkT", row))
                    for f in fills:
                        pe.wait_ge(*drained("D", f"s{f}", row))
                        dst = psum("D", f"s{f}")
                        for n, h in enumerate(D_HEADS[f]):
                            r = slice(32 * (h % 4), 32 * (h % 4) + DH)
                            last = pe.matmul(dst[:, n * P:(n + 1) * P], d_qkT[r, h // 4, :], d_qkT[r, 3 + h // 4, :],
                                             start=True, stop=True)
                        last.then_inc(full[bank_of("D", f"s{f}")], 1)
                return step

            def d_context(row):
                pe.wait_ge(*made("D", "pT", row))
                pe.wait_ge(*made("D", "v", row))
                pe.wait_ge(*drained("D", "c", row))
                dst = psum("D", "c")
                for h in range(NH):
                    last = pe.matmul(dst[:, h * DH:(h + 1) * DH], d_pT[:, h, :], d_vs[:, h * DH:(h + 1) * DH],
                                     start=True, stop=True)
                last.then_inc(full[bank_of("D", "c")], 1)

            def d_tr(src, needs, fill):
                def step(row):
                    pe.wait_ge(*made("D", needs, row))
                    transpose_pair("D", row, src, fill)
                return step

            def pair_product(lhs, w, needs, fill):
                def step(row):
                    pe.wait_ge(*made("D", needs, row))
                    pe.wait_ge(*drained("D", fill, row))
                    dst = psum("D", fill)
                    pe.matmul(dst[:, 0:H], lhs[0:HC, 0, :], w[0:HC, 0, :], start=True, stop=False)
                    pe.matmul(dst[:, 0:H], lhs[:, 1, :], w[:, 1, :], start=False, stop=True).then_inc(full[bank_of("D", fill)], 1)
                return step

            def d_hidden(row):
                pe.wait_ge(*made("D", "z2T", row))
                for g in range(2):
                    pe.wait_ge(*drained("D", f"f{g}", row))
                    dst = psum("D", f"f{g}")
                    for k in range(3):
                        fs = slice((3 * g + k) * P, (3 * g + k + 1) * P)
                        o = dst[:, k * P:(k + 1) * P]
                        pe.matmul(o, d_fc1[:, 0, fs], d_z2T[:, 0, :], start=True, stop=False)
                        last = pe.matmul(o, d_fc1[:, 1, fs], d_z2T[:, 1, :], start=False, stop=True)
                    last.then_inc(full[bank_of("D", f"f{g}")], 1)

            def d_mlp_out(row):
                pe.wait_ge(*made("D", "fT", row))
                pe.wait_ge(*drained("D", "o", row))
                dst = psum("D", "o")
                for f in range(NFC):
                    last = pe.matmul(dst[:, 0:H], d_fT[:, f, :], d_fc2[:, f, :], start=(f == 0), stop=(f == NFC - 1))
                last.then_inc(full[bank_of("D", "o")], 1)

            steps = {}
            for l, lane in enumerate(TOK):
                steps[lane, "tr"] = tok_tr(lane)
                steps[lane, "qkv"] = tok_qkv(lane, l)
                steps[lane, "tc"] = tok_tc(lane)
                steps[lane, "y"] = tok_y(lane, l)
                steps[lane, "m"] = tok_m(lane)
                steps[lane, "ff"] = tok_ff(lane, l)
                steps[lane, "o"] = tok_o(lane, l)
            steps |= {("B", "g"): gate_tr, ("B", "u"): gate, ("B", "hs"): window_sum,
                      ("C", "z"): c_z_tr, ("C", "qk"): c_qk, ("C", "v"): c_values, ("C", "sA"): c_scores((0, 1)),
                      ("C", "sB"): c_scores((2, 3)), ("C", "p"): transpose_p("C", c_p),
                      ("C", "c"): c_context, ("C", "y"): c_out,
                      ("D", "norm_z"): d_qkv, ("D", "e"): router_e, ("D", "h1"): router_h1,
                      ("D", "h2"): router_h2, ("D", "lg"): router_logits, ("D", "qk"): d_heads,
                      ("D", "sA"): d_scores((0, 1)), ("D", "sB"): d_scores((2, 3)),
                      ("D", "p"): transpose_p("D", d_p), ("D", "c"): d_context,
                      ("D", "t"): d_tr(d_ctx, "ctx", "t"), ("D", "y"): pair_product(d_cT, d_o, "cT", "y"),
                      ("D", "z2"): d_tr(d_z, "z2", "z2"), ("D", "ff"): d_hidden, ("D", "o"): d_mlp_out,
                      ("D", "ot"): d_tr(d_out, "out", "ot"), ("D", "dn"): pair_product(d_oT, d_down, "oT", "dn"),
                      ("D", "dt"): d_tr(d_dn, "dn", "dt"), ("D", "up"): pair_product(d_oT, d_up, "dT", "up")}
            run(pe, steps)

        @block.scalar
        def _(act):
            act.wait_ge(weights_loaded, 16 * len(loads))
            act.wait_ge(const_ready, 3)

            def scale_rows(lane, row, dst, fills, name, g, b):
                for c, fill in enumerate(fills):
                    act.wait_ge(*written(lane, fill, row))
                    act.activation(dst[0:HC, c, :], psum(lane, fill)[0:HC, 0:NSLOT * P], ACT.Identity,
                                                    bias=col(b, HC, c), scale=col(g, HC, c)).then_inc(signal[lane][name], 1)

            def tok_tr(lane, g, b):
                def step(row):
                    act.wait_ge(*written(lane, "v2", row, back=1))
                    if lane == "B":
                        act.wait_ge(*written("B", "u2", row, back=1))
                    scale_rows(lane, row, xT[lane], ("tr0", "tr1"), "xT", g, b)
                return step

            def tok_qkv(lane):
                def step(row):
                    act.wait_ge(*made(lane, "qkp", row, back=1))
                    act.wait_ge(*made(lane, "pvp", row, back=1))
                    act.wait_ge(*made(lane, "z2", row, back=1))
                    if lane == "B":
                        act.wait_ge(*written("B", "hs", row, back=1))
                    for j in range(NSLOT):
                        act.wait_ge(*written(lane, f"qk{j}", row))
                        act.copy(qkv[lane][:, j, 0:2 * H], psum(lane, f"qk{j}")[:, 0:2 * H]).then_inc(signal[lane]["qk"], 1)
                    act.wait_ge(*written(lane, "v01", row))
                    act.copy(qkv[lane][:, 0:2, 2 * H:], psum(lane, "v01")[:, 0:2 * H]
                                             .rearrange("p (j f) -> p j f", j=2)).then_inc(signal[lane]["v"], 1)
                    act.wait_ge(*written(lane, "v2", row))
                    act.copy(qkv[lane][:, 2, 2 * H:], psum(lane, "v2")[:, 0:H]).then_inc(signal[lane]["v"], 1)
                return step

            def tok_exp(lane):
                def step(row):
                    act.wait_ge(*made(lane, "shifted", row))
                    act.activation(pr[lane][:, :], sc[lane][:, :], ACT.Exp).then_inc(signal[lane]["ex"], 1)
                return step

            def tok_tc(lane):
                def step(row):
                    act.wait_ge(*written(lane, "o2", row, back=1))
                    for c in range(2):
                        act.wait_ge(*written(lane, f"c{c}", row))
                        act.copy(cT[lane][:, c, :], psum(lane, f"c{c}")[0:HC, 0:NSLOT * P]).then_inc(signal[lane]["cT"], 1)
                return step

            def tok_m(lane, l):
                def step(row):
                    if lane == "A":
                        act.wait_ge(*written("B", "f5", row, back=1))
                    else:
                        act.wait_ge(*written("A", "f5", row))
                    for c, part in enumerate((x1_high, x1_both)):
                        g, b = col(f"x1_g{l}", P, c), col(f"x1_b{l}", P, c)
                        src = psum(lane, f"m{c}")[:, 0:NSLOT * P]
                        act.wait_ge(*written(lane, f"m{c}", row))
                        act.activation(x1f[:, c, :], src, ACT.Identity, bias=b, scale=g)
                        act.activation(part[:, :], src, ACT.Identity, bias=b, scale=g
                                       ).then_inc(signal[lane]["x1T"], 1)
                return step

            def tok_ff(lane, l):
                def step(row):
                    for f in range(NFC):
                        act.wait_ge(*written(lane, f"f{f}", row))
                        act.activation(fT[lane][:, f, :], psum(lane, f"f{f}")[:, 0:NSLOT * P],
                                                        ACT.Gelu, bias=col(f"b1{l}", P, f)).then_inc(signal[lane]["fT"], 1)
                return step

            def gate_tr(row):
                act.wait_ge(*written("B", "o2", row))
                scale_rows("B", row, xT["B"], ("g0", "g1"), "gT", "ln2_g1", "ln2_b1")

            def gate_tanh(row):
                act.wait_ge(*written("B", "u01", row))
                act.activation(tanh[:, 0:2, :], psum("B", "u01")[:, 0:2 * H].rearrange("p (j f) -> p j f", j=2),
                               ACT.Tanh, scale=0.5).then_inc(signal["B"]["th"], 1)
                act.wait_ge(*written("B", "u2", row))
                act.activation(tanh[:, 2, :], psum("B", "u2")[:, 0:H], ACT.Tanh, scale=0.5
                               ).then_inc(signal["B"]["th"], 1)

            def c_z_tr(row):
                act.wait_ge(*written("C", "z", row))
                act.wait_ge(*written("C", "v1", row, back=1))
                act.copy(c_zT[0:HC, :, :], psum("C", "z")[0:HC, 0:2 * P].rearrange("p (c t) -> p c t", c=2)).then_inc(signal["C"]["zT"], 1)

            def c_qk(row):
                act.wait_ge(*written("C", "c1", row, back=1))
                for g in range(3):
                    act.wait_ge(*written("C", f"qk{g}", row))
                    act.copy(c_qkT[:, 4 * g:4 * g + 4, :], psum("C", f"qk{g}")[:, :]
                                              .rearrange("p (k t) -> p k t", k=4)).then_inc(signal["C"]["qkT"], 1)

            def c_values(row):
                for g in range(2):
                    act.wait_ge(*written("C", f"v{g}", row))
                    act.copy(c_v[:, g * 384:(g + 1) * 384], psum("C", f"v{g}")[:, 0:384]).then_inc(signal["C"]["v"], 1)

            def exps(lane, fills, heads, probs, nm, sums, scale):
                def step(row):
                    if fills[0] == 0:
                        act.wait_ge(*written(lane, "y", row, back=1))
                        if lane == "D":
                            act.wait_ge(*written(lane, "o", row, back=1))
                    for f in fills:
                        act.wait_ge(*made(lane, "nm", row, f + 1))
                        for n, h in enumerate(heads[f]):
                            last = act.activation(probs[:, h, :], psum(lane, f"s{f}")[:, n * P:(n + 1) * P], ACT.Exp,
                                                  scale=scale, bias=nm[:, 1, 3 * f + n:3 * f + n + 1],
                                                  accum_out=sums[:, 0, h:h + 1])
                        last.then_inc(signal[lane]["ex"], 1)
                return step

            def copy_pT(lane, dst):
                def step(row):
                    for g in range(3):
                        act.wait_ge(*written(lane, f"p{g}", row))
                        act.copy(dst[:, 4 * g:4 * g + 4, :], psum(lane, f"p{g}")[:, :]
                                                  .rearrange("p (k t) -> p k t", k=4)).then_inc(signal[lane]["pT"], 1)
                return step

            def c_context(row):
                for g in range(2):
                    act.wait_ge(*written("C", f"c{g}", row))
                    act.copy(c_cT[:, 3 * g:3 * g + 3, :], psum("C", f"c{g}")[:, 0:384]
                                             .rearrange("p (k t) -> p k t", k=3)).then_inc(signal["C"]["cT"], 1)

            def d_norm_z(row):
                act.wait_ge(*written("D", "z", row))
                act.wait_ge(*written("D", "up", row, back=1))
                for c in range(2):
                    last = act.activation(d_zrT[:, c, :], psum("D", "z")[0:HC, c * P:(c + 1) * P], ACT.Identity,
                                          bias=col("r_b", HC, c), scale=col("r_g", HC, c))
                last.then_inc(signal["D"]["zrT"], 1)
                for c in range(2):
                    last = act.activation(d_zT[0:HC, c, :], psum("D", "z")[0:HC, c * P:(c + 1) * P], ACT.Identity,
                                          bias=col("a_b", HC, c), scale=col("a_g", HC, c))
                last.then_inc(signal["D"]["zT"], 1)

            def router_e(row):
                act.wait_ge(*written("D", "e", row))
                act.wait_ge(*written("D", "h1", row, back=1))
                act.activation(d_eT[:, :], psum("D", "e")[:, 0:P], ACT.Gelu, bias=col("r_in_b", P)).then_inc(signal["D"]["eT"], 1)

            def router_h1(row):
                act.wait_ge(*made("D", "hb", row))
                act.wait_ge(*written("D", "h2", row, back=1))
                act.activation(d_h1T[:, :], psum("D", "h1")[:, 0:P], ACT.Gelu, bias=hbias).then_inc(signal["D"]["h1T"], 1)

            def router_h2(row):
                act.wait_ge(*written("D", "h2", row))
                act.wait_ge(*written("D", "lg", row, back=1))
                act.activation(d_h2T[0:RHD // 2, :], psum("D", "h2")[0:RHD // 2, 0:P], ACT.Gelu,
                                                bias=col("r_o2_b", RHD // 2)).then_inc(signal["D"]["h2T"], 1)

            def d_heads(row):
                act.wait_ge(*written("D", "c", row, back=1))
                for g in range(2):
                    act.wait_ge(*written("D", f"qk{g}", row))
                    act.copy(d_qkT[:, 3 * g:3 * g + 3, :], psum("D", f"qk{g}")[:, 0:384]
                                              .rearrange("p (k t) -> p k t", k=3)).then_inc(signal["D"]["qkT"], 1)
                act.wait_ge(*written("D", "v", row))
                act.copy(d_vs[:, :], psum("D", "v")[:, 0:H]).then_inc(signal["D"]["v"], 1)

            def copy_pair(fill, dst, name, after):
                def step(row):
                    act.wait_ge(*written("D", fill, row))
                    act.wait_ge(*written("D", after, row, back=1))
                    act.copy(dst[0:HC, :, :], psum("D", fill)[0:HC, 0:2 * P]
                                             .rearrange("p (c t) -> p c t", c=2)).then_inc(signal["D"][name], 1)
                return step

            def d_z2(row):
                act.wait_ge(*written("D", "z2", row))
                for c in range(2):
                    last = act.activation(d_z2T[:, c, :], psum("D", "z2")[0:HC, c * P:(c + 1) * P], ACT.Identity,
                                          bias=col("f_b", HC, c), scale=col("f_g", HC, c))
                last.then_inc(signal["D"]["z2T"], 1)

            def d_hidden(row):
                for g in range(2):
                    act.wait_ge(*written("D", f"f{g}", row))
                    for k in range(3):
                        last = act.activation(d_fT[:, 3 * g + k, :], psum("D", f"f{g}")[:, k * P:(k + 1) * P], ACT.Gelu,
                                              bias=col("fc1_b", P, 3 * g + k))
                    last.then_inc(signal["D"]["fT"], 1)

            steps = {}
            for l, lane in enumerate(TOK):
                g, b = (("emb_g", "emb_b"), ("ln2_g0", "ln2_b0"))[l]
                steps[lane, "tr"] = tok_tr(lane, g, b)
                steps[lane, "qkv"] = tok_qkv(lane)
                steps[lane, "soft"] = tok_exp(lane)
                steps[lane, "tc"] = tok_tc(lane)
                steps[lane, "m"] = tok_m(lane, l)
                steps[lane, "ff"] = tok_ff(lane, l)
            steps |= {("B", "g"): gate_tr, ("B", "u"): gate_tanh, ("C", "z"): c_z_tr, ("C", "qk"): c_qk, ("C", "v"): c_values,
                      ("C", "sA"): exps("C", (0, 1), C_HEADS, c_p, c_nm, c_sum, ATT_SCALE),
                      ("C", "sB"): exps("C", (2, 3), C_HEADS, c_p, c_nm, c_sum, ATT_SCALE),
                      ("C", "p"): copy_pT("C", c_qkT), ("C", "c"): c_context,
                      ("D", "norm_z"): d_norm_z, ("D", "e"): router_e, ("D", "h1"): router_h1,
                      ("D", "h2"): router_h2, ("D", "qk"): d_heads,
                      ("D", "sA"): exps("D", (0, 1), D_HEADS, d_p, d_nm, d_sum, TOK_SCALE),
                      ("D", "sB"): exps("D", (2, 3), D_HEADS, d_p, d_nm, d_sum, TOK_SCALE),
                      ("D", "p"): copy_pT("D", d_pT), ("D", "t"): copy_pair("t", d_cT, "cT", "y"),
                      ("D", "z2"): d_z2, ("D", "ff"): d_hidden,
                      ("D", "ot"): copy_pair("ot", d_oT, "oT", "up"), ("D", "dt"): copy_pair("dt", d_oT, "dT", "dn")}
            run(act, steps)

        @block.vector
        def _(dve):
            chains = {lane: Chain(sem(f"{lane}_dve_chain")) for lane in LAG}
            for l in TOK:
                dve.memset(xT[l][HC:HC + 1, :, :], 1.0)
            for t in (c_zT, d_zT):
                dve.memset(t[HC:HC + 1, :, :], 1.0)
            dve.memset(d_h2T[RHD // 2:RHD // 2 + 1, :], 1.0).then_inc(const_ready, 1)
            dve.wait_ge(weights_loaded, 16 * len(loads))
            dve.wait_ge(const_ready, 3)
            dve.tensor_scalar(mask[:, :], ids[:, :], 0.0, None, ALU.is_gt).then_inc(masks_ready, 1)
            dve.tensor_copy(kind[:, :], kinds[:, :]).then_inc(masks_ready, 1)
            dve.tensor_tensor(pos2[:, :], pos2[:, :], type2[:, 0, :], ALU.add).then_inc(masks_ready, 1)
            dve.tensor_tensor(type2[:, 1, :], type2[:, 1, :], type2[:, 0, :], ALU.subtract).then_inc(masks_ready, 1)
            dve.wait_ge(masks_ready, 4)
            m3 = mask[:, :].rearrange("p (r j) -> p r j", j=NSLOT)
            g3 = gate_mask[:, :].rearrange("p (r j) -> p r j", j=NSLOT)
            dve.tensor_scalar(g3[:, :, 1], m3[:, :, 1], 0.5, None, ALU.mult).then_inc(masks_ready, 1)
            dve.wait_ge(masks_ready, 5)
            for j in (0, 2):
                dve.tensor_tensor(g3[:, :, j], m3[:, :, j], g3[:, :, 1], ALU.mult).then_inc(masks_ready, 1)
            dve.wait_ge(masks_ready, 7)
            dve.tensor_scalar(m3[:, :, 1], m3[:, :, 1], 0.0, None, ALU.mult).then_inc(masks_ready, 1)
            for j in (0, 2):
                dve.tensor_scalar(m3[:, :, j], m3[:, :, j], BIG, -BIG, ALU.mult, ALU.add).then_inc(masks_ready, 1)
            dve.tensor_tensor(shift[:, 0:4, :], shift[:, 0:4, :], out_bias, ALU.add).then_inc(masks_ready, 1)
            for l, lane in enumerate(TOK):
                raw = w1_raw[lane]
                dve.tensor_copy(w1_high[l][:, :], raw[:, 0, :]).then_inc(masks_ready, 1)
                dve.tensor_copy(w1_both[l][:, :], raw[:, 1, :]).then_inc(masks_ready, 1)
            dve.wait_ge(masks_ready, 15)
            for l, lane in enumerate(TOK):
                raw, r = w1_raw[lane], high_rows[l]
                dve.tensor_tensor(w1_low[l][:, :], raw[:, 0, :], w1_high[l][:, :].bitcast(F32), ALU.subtract)
                dve.tensor_tensor(w1_rest[r, :], raw[r, 1, :], w1_both[l][r, :].bitcast(F32), ALU.subtract
                                  ).then_inc(masks_ready, 1)
            dve.wait_ge(masks_ready, 17)

            def statistics(lane, n, row, sources, eps):
                st, mv, ve, _ = lnst[lane, n]
                chain = chains[lane]
                for k, y in enumerate(sources):
                    dve.bn_stats(st[:, k, :], y).then_inc(chain.sem, chain.tick())
                for k in range(len(sources)):
                    if k == 0:
                        dve.wait_ge(chain.sem, chain.value(row))
                        dve.memset(scratch[:, 0:1], 0.0)
                    dve.bn_aggr(mv[:, k, :], st[:, k, :]).then_inc(chain.sem, chain.tick())
                dve.wait_ge(chain.sem, chain.value(row))
                dve.tensor_scalar(ve[:, :], mv[:, :, 1], eps, None, ALU.add).then_inc(signal[lane]["ve" + n], 1)

            def normalize(lane, n, k, dst, src):
                _, mv, _, rs = lnst[lane, n]
                return dve.tensor_scalar(dst, src, mv[:, k, 0:1], rs[:, k:k + 1], ALU.subtract, ALU.mult)

            def emb_stats(row):
                dve.wait_ge(*made("E", "emb", row))
                statistics("E", "", row, [emb[:, j, :] for j in range(NSLOT)], EPS_TOK)

            def emb_norm(row):
                dve.wait_ge(*made("E", "rs", row))
                for j in range(NSLOT):
                    last = normalize("E", "", j, emb[:, j, :], emb[:, j, :])
                last.then_inc(signal["A"]["zin"], 1)

            def tok_soft(lane):
                chain = chains[lane]

                def step(row):
                    pv = prod[lane].rearrange("p (i m d) -> p i m d", i=NSLOT, d=DH)
                    s = sc[lane][:, :].rearrange("p (i m) -> p i m", i=NSLOT)
                    dve.wait_ge(*made(lane, "ctx", row, back=1))
                    for i in range(NSLOT):
                        dve.wait_ge(*made(lane, "qkp", row, i + 1))
                        dve.tensor_reduce(s[:, i, :], pv[:, i], AX.X, ALU.add).then_inc(chain.sem, chain.tick())
                    dve.wait_ge(chain.sem, chain.value(row))
                    s4 = sc[lane][:, :].rearrange("p (i k h) -> p i k h", i=NSLOT, k=NSLOT)
                    for k in range(NSLOT):
                        bias = att_bias[:, bass.ds(row.times(NSLOT, k), 1)]
                        dve.tensor_scalar(s4[:, :, k, :], s4[:, :, k, :], TOK_SCALE, bias, ALU.mult, ALU.add).then_inc(chain.sem, chain.tick())
                    dve.wait_ge(chain.sem, chain.value(row))
                    m = mx[lane][:, :].rearrange("p (i h) -> p i h", i=NSLOT)
                    dve.tensor_reduce(m, s4.rearrange("p i k h -> p i h k"), AX.X, ALU.max).then_inc(chain.sem, chain.tick())
                    dve.wait_ge(chain.sem, chain.value(row))
                    dve.tensor_tensor(s4, s4, m.unsqueeze(2).to_broadcast([P, NSLOT, NSLOT, NH]),
                                                            ALU.subtract).then_inc(signal[lane]["shifted"], 1)
                return step

            def tok_pv(lane):
                chain = chains[lane]

                def step(row):
                    dve.wait_ge(*made(lane, "ex", row))
                    p4 = pr[lane][:, :].rearrange("p (i k h) -> p i k h", i=NSLOT, k=NSLOT)
                    m = mx[lane][:, :].rearrange("p (i h) -> p i h", i=NSLOT)
                    dve.tensor_reduce(m, p4.rearrange("p i k h -> p i h k"), AX.X, ALU.add).then_inc(chain.sem, chain.tick())
                    dve.wait_ge(chain.sem, chain.value(row))
                    dve.reciprocal(mx[lane][:, :], mx[lane][:, :]).then_inc(chain.sem, chain.tick())
                    dve.wait_ge(chain.sem, chain.value(row))
                    dve.tensor_tensor(p4, p4, m.unsqueeze(2).to_broadcast([P, NSLOT, NSLOT, NH]), ALU.mult).then_inc(signal[lane]["p"], 1)
                return step

            def tok_ctx(lane):
                chain = chains[lane]

                def step(row):
                    pv = prod[lane].rearrange("p (i k f) -> p i k f", i=NSLOT, k=NSLOT)
                    c = ctxt[lane]
                    dve.wait_ge(*written(lane, "m1", row, back=1))
                    if lane == "A":
                        dve.wait_ge(*written("B", "tr1", row, back=1))
                        dve.wait_ge(*made("B", "rg", row, back=1))
                    else:
                        dve.wait_ge(*written("B", "g1", row, back=1))
                        dve.wait_ge(*made("B", "rgg", row, back=1))
                    dve.wait_ge(*made(lane, "pvp", row))
                    dve.tensor_tensor(c[:, :, :], pv[:, :, 0, :], pv[:, :, 1, :], ALU.add).then_inc(chain.sem, chain.tick())
                    dve.wait_ge(chain.sem, chain.value(row))
                    dve.tensor_tensor(c[:, :, :], c[:, :, :], pv[:, :, 2, :], ALU.add).then_inc(signal[lane]["ctx"], 1)
                return step

            def tok_ln(lane, n, fills, added, residual, ready):
                def step(row):
                    dve.wait_ge(*made(lane, ready, row))
                    x = residual[lane]
                    dve.wait_ge(*written(lane, fills[0], row))
                    dve.tensor_tensor(x[:, 0:2, :], psum(lane, fills[0])[:, 0:2 * H].rearrange("p (j f) -> p j f", j=2),
                                      x[:, 0:2, :], ALU.add).then_inc(signal[lane][added], 1)
                    dve.wait_ge(*written(lane, fills[1], row))
                    dve.tensor_tensor(x[:, 2, :], psum(lane, fills[1])[:, 0:H], x[:, 2, :], ALU.add
                                      ).then_inc(signal[lane][added], 1)
                    dve.wait_ge(*made(lane, added, row))
                    statistics(lane, n, row, [x[:, j, :] for j in range(NSLOT)], EPS_TOK)
                return step

            def tok_norm(lane, n, residual):
                def step(row):
                    dve.wait_ge(*made(lane, "rs" + n, row))
                    if n == "2":
                        dve.wait_ge(*made(lane, "rg1", row))
                    for j in range(NSLOT):
                        last = normalize(lane, n, j, ctxt[lane][:, j, :], residual[lane][:, j, :])
                    if n == "1":
                        for j in range(NSLOT):
                            src = residual[lane][:, j, P:H].unsqueeze(1).to_broadcast([P, 2, H - P])
                            last = normalize(lane, n, j, z1_twice[lane][:, j, :].rearrange("p (c f) -> p c f", c=2), src)
                    last.then_inc(signal[lane]["z" + n], 1)
                return step

            def tok_low(lane, l):
                low = low_rows[l]

                def step(row):
                    dve.wait_ge(*made(lane, "x1T", row, 1))
                    dve.tensor_tensor(x1_low[:, :], x1f[:, 0, :], x1_high[:, :].bitcast(F32), ALU.subtract
                                      ).then_inc(signal[lane]["x1lo"], 1)
                    dve.wait_ge(*made(lane, "x1T", row, 2))
                    dve.tensor_tensor(x1_both[low, :], x1f[low, 1, :], x1_both[low, :].bitcast(F32), ALU.subtract
                                      ).then_inc(signal[lane]["x1lo"], 1)
                return step

            def gate_product(row):
                dve.wait_ge(*made("B", "th", row))
                dve.wait_ge(*made("B", "resg", row))
                dve.scalar_tensor_tensor(out=gated, in0=tanh, scalar=1.0, in1=xgate, op0=ALU.add, op1=ALU.mult
                                         ).then_inc(signal["B"]["gx"], 1)
                dve.wait_ge(*made("B", "gx", row))
                for j in range(NSLOT):
                    last = dve.tensor_scalar(gated[:, j, :], gated[:, j, :],
                                             gate_mask[:, bass.ds(row.times(NSLOT, j), 1)], None, ALU.mult)
                last.then_inc(signal["B"]["gm"], 1)

            def window_sum(row):
                chain = chains["B"]
                dve.scalar_tensor_tensor(out=hpre[:, :], in0=type2[:, 1, :],
                                                    scalar=kind[:, bass.ds(row.times(1, 0), 1)], in1=pos2[:, :],
                                                    op0=ALU.mult, op1=ALU.add).then_inc(chain.sem, chain.tick())
                dve.wait_ge(*written("B", "hs", row))
                dve.wait_ge(chain.sem, chain.value(row))
                dve.tensor_tensor(hpre[:, :], psum("B", "hs")[:, 0:H], hpre[:, :], ALU.add).then_inc(signal["B"]["hsum"], 1)

            def norm_stats(row):
                dve.wait_ge(*made("B", "hsum", row))
                statistics("B", "3", row, [hpre[:, :]], EPS_TOK)

            def norm_out(row):
                chain = chains["B"]
                dve.wait_ge(*made("B", "rs3", row))
                normalize("B", "3", 0, hpre[:, :], hpre[:, :]).then_inc(signal["B"]["z3"], 1)
                dve.wait_ge(*made("B", "z3", row))
                dve.tensor_tensor(hpre[:, :], hpre[:, :], norm_gb[:, 0, :], ALU.mult).then_inc(signal["B"]["zg"], 1)
                dve.wait_ge(*made("B", "zg", row))
                dve.wait_ge(*made("B", "h0b", row, back=1))
                dve.tensor_tensor(h0[:, :], hpre[:, :], norm_gb[:, 1, :], ALU.add).then_inc(signal["B"]["h0"], 1)

            def c_stats(row):
                dve.wait_ge(*made("B", "h0", row))
                statistics("C", "", row, [h0[:, :]], EPS)

            def c_norm(row):
                dve.wait_ge(*made("C", "rs", row))
                dve.wait_ge(*written("C", "z", row, back=1))
                normalize("C", "", 0, c_z[:, :], h0[:, :]).then_inc(signal["C"]["z"], 1)

            def maxima(lane, fills, nm, scale):
                def step(row):
                    chain = chains[lane]
                    for f in fills:
                        dve.wait_ge(*written(lane, f"s{f}", row))
                        dve.wait_ge(*made(lane, "ex", row, f + 1, back=1))
                        cs = slice(3 * f, 3 * f + 3)
                        dve.tensor_reduce(nm[:, 0, cs], psum(lane, f"s{f}")[:, 0:384]
                                                     .rearrange("p (h t) -> p h t", h=3), AX.X, ALU.max, negate=True).then_inc(chain.sem, chain.tick())
                        dve.wait_ge(chain.sem, chain.value(row))
                        dve.tensor_scalar(nm[:, 1, cs], nm[:, 0, cs], scale, None, ALU.mult).then_inc(signal[lane]["nm"], 1)
                return step

            def inverse_sums(lane, sums):
                def step(row):
                    dve.wait_ge(*made(lane, "ex", row))
                    dve.reciprocal(sums[:, 1, :], sums[:, 0, :]).then_inc(chains[lane].sem, chains[lane].tick())
                return step

            def c_probabilities(row):
                chain = chains["C"]
                dve.wait_ge(*made("C", "ex", row))
                dve.reciprocal(c_sum[:, 1, :], c_sum[:, 0, :]).then_inc(chain.sem, chain.tick())
                dve.wait_ge(chain.sem, chain.value(row))
                for g in range(3):
                    hs = slice(4 * g, 4 * g + 4)
                    dve.tensor_tensor(c_p[:, hs, :], c_p[:, hs, :], c_sum[:, 1, hs].unsqueeze(2).to_broadcast([P, 4, P]),
                                      ALU.mult).then_inc(signal["C"]["pn"], 1)

            def c_out(row):
                dve.wait_ge(*written("C", "y", row))
                dve.wait_ge(*made("B", "h0b", row))
                dve.wait_ge(*made("D", "x", row, back=1))
                dve.tensor_tensor(h1[:, :], psum("C", "y")[:, 0:H], h0b[:, :], ALU.add).then_inc(signal["C"]["h1"], 1)

            def d_stats_x(row):
                dve.wait_ge(*made("C", "h1", row))
                statistics("D", "x", row, [h1[:, :]], EPS)

            def d_norm_x(row):
                dve.wait_ge(*made("D", "rsx", row))
                dve.tensor_copy(d_h1[:, :], h1[:, :]).then_inc(chains["D"].sem, chains["D"].tick())
                normalize("D", "x", 0, d_x[:, :], h1[:, :]).then_inc(signal["D"]["x"], 1)

            def d_stats_z(row):
                dve.wait_ge(*made("D", "x", row))
                statistics("D", "", row, [d_x[:, :]], EPS)

            def d_norm_z(row):
                dve.wait_ge(*made("D", "rs", row))
                normalize("D", "", 0, d_z[:, :], d_x[:, :]).then_inc(signal["D"]["z"], 1)

            def router_mean(row):
                chain = chains["D"]
                dve.wait_ge(*made("D", "eT", row))
                dve.tensor_reduce(gsum, d_eT[:, 1:P], AX.X, ALU.add).then_inc(chain.sem, chain.tick())
                dve.wait_ge(chain.sem, chain.value(row))
                dve.tensor_scalar(gmean, gsum, 1.0 / (P - 1), None, ALU.mult).then_inc(signal["D"]["gs"], 1)

            def router_h1(row):
                dve.wait_ge(*written("D", "h1", row))
                dve.tensor_tensor(hbias, psum("D", "h1")[:, P:P + 1], col("r_o1_b", P), ALU.add).then_inc(signal["D"]["hb"], 1)

            def router_bits(row):
                chain = chains["D"]
                dve.wait_ge(*written("D", "lg", row))
                dve.tensor_copy(logits, psum("D", "lg")[:, 0:4]).then_inc(signal["D"]["lgs"], 1)
                dve.wait_ge(*made("D", "lgs", row))
                dve.tensor_tensor(bits, logits[:, 1:4:2], logits[:, 0:4:2], ALU.is_gt).then_inc(chain.sem, chain.tick())
                dve.wait_ge(chain.sem, chain.value(row))
                dve.tensor_tensor(bits, bits, first[:, :], ALU.max).then_inc(chain.sem, chain.tick())
                dve.wait_ge(chain.sem, chain.value(row))
                dve.tensor_scalar(nbits, bits, -1.0, 1.0, ALU.mult, ALU.add).then_inc(chain.sem, chain.tick())
                dve.wait_ge(chain.sem, chain.value(row))
                dve.tensor_tensor(sel[:, 0:1], nbits[:, 0:1], nbits[:, 1:2], ALU.mult).then_inc(chain.sem, chain.tick())
                dve.tensor_tensor(sel[:, 1:2], nbits[:, 0:1], bits[:, 1:2], ALU.mult).then_inc(chain.sem, chain.tick())
                dve.tensor_tensor(sel[:, 2:3], bits[:, 0:1], nbits[:, 1:2], ALU.mult).then_inc(signal["D"]["sel"], 1)

            def d_context(row):
                dve.wait_ge(chains["D"].sem, chains["D"].value(row))
                dve.wait_ge(*written("D", "c", row))
                r = d_sum[:, 1, :].unsqueeze(2).to_broadcast([P, NH, DH])
                dve.tensor_tensor(d_ctx[:, :].rearrange("p (h e) -> p h e", h=NH),
                                                   psum("D", "c")[:, 0:H].rearrange("p (h e) -> p h e", h=NH), r, ALU.mult).then_inc(signal["D"]["ctx"], 1)

            def d_residual(row):
                dve.wait_ge(*written("D", "y", row))
                dve.wait_ge(*made("D", "sel", row))
                dve.scalar_tensor_tensor(out=d_h[:, :], in0=psum("D", "y")[:, 0:H], scalar=bits[:, 0:1],
                                                         in1=d_x[:, :], op0=ALU.mult, op1=ALU.add).then_inc(signal["D"]["hd"], 1)

            def d_stats_2(row):
                dve.wait_ge(*made("D", "hd", row))
                statistics("D", "2", row, [d_h[:, :]], EPS)

            def d_norm_2(row):
                dve.wait_ge(*made("D", "rs2", row))
                normalize("D", "2", 0, d_z[:, :], d_h[:, :]).then_inc(signal["D"]["z2"], 1)

            def d_mlp_out(row):
                dve.wait_ge(*written("D", "o", row))
                dve.tensor_tensor(d_ff[:, :], psum("D", "o")[:, 0:H], fc2_b[:, :], ALU.add).then_inc(signal["D"]["od"], 1)
                dve.wait_ge(*made("D", "od", row))
                dve.wait_ge(*made("D", "stored", row, back=1))
                dve.scalar_tensor_tensor(out=d_out[:, :], in0=d_ff[:, :], scalar=bits[:, 1:2],
                                                          in1=d_h[:, :], op0=ALU.mult, op1=ALU.add).then_inc(signal["D"]["out"], 1)

            def d_down_masked(row):
                dve.wait_ge(*written("D", "dn", row))
                for k in range(NSLOT):
                    last = dve.tensor_scalar(d_dn[:, k * RANK:(k + 1) * RANK],
                                             psum("D", "dn")[:, k * RANK:(k + 1) * RANK], sel[:, k:k + 1], None, ALU.mult)
                last.then_inc(signal["D"]["dn"], 1)

            def d_final(row):
                chain = chains["D"]
                dve.wait_ge(*written("D", "up", row))
                dve.tensor_tensor(d_out[:, :], psum("D", "up")[:, 0:H], d_out[:, :], ALU.add).then_inc(chain.sem, chain.tick())
                dve.wait_ge(chain.sem, chain.value(row))
                dve.tensor_tensor(d_out[:, :], d_out[:, :], d_h1[:, :], ALU.add).then_inc(signal["D"]["fin"], 1)

            steps = {"chains": {lane: (chains[lane],) for lane in LAG}}
            for lane in TOK:
                steps[lane, "soft"] = tok_soft(lane)
                steps[lane, "pv"] = tok_pv(lane)
                steps[lane, "ctx"] = tok_ctx(lane)
                steps[lane, "ln1"] = tok_ln(lane, "1", ("y01", "y2"), "ya", xres, "res")
                steps[lane, "norm1"] = tok_norm(lane, "1", xres)
                steps[lane, "m"] = tok_low(lane, TOK.index(lane))
                steps[lane, "ln2"] = tok_ln(lane, "2", ("o01", "o2"), "oa", x1res, "res1")
                steps[lane, "norm2"] = tok_norm(lane, "2", x1res)
            steps |= {("E", "stats"): emb_stats, ("E", "norm"): emb_norm, ("B", "u"): gate_product,
                      ("B", "hs"): window_sum, ("B", "ln3"): norm_stats, ("B", "norm3"): norm_out,
                      ("C", "ln"): c_stats, ("C", "norm"): c_norm,
                      ("C", "sA"): maxima("C", (0, 1), c_nm, ATT_SCALE), ("C", "sB"): maxima("C", (2, 3), c_nm, ATT_SCALE),
                      ("C", "p"): c_probabilities, ("C", "y"): c_out,
                      ("D", "ln_x"): d_stats_x, ("D", "norm_x"): d_norm_x, ("D", "ln_z"): d_stats_z,
                      ("D", "norm_z"): d_norm_z, ("D", "e"): router_mean, ("D", "h1"): router_h1,
                      ("D", "lg"): router_bits,
                      ("D", "sA"): maxima("D", (0, 1), d_nm, TOK_SCALE), ("D", "sB"): maxima("D", (2, 3), d_nm, TOK_SCALE),
                      ("D", "p"): inverse_sums("D", d_sum), ("D", "c"): d_context, ("D", "y"): d_residual,
                      ("D", "ln2"): d_stats_2, ("D", "norm2"): d_norm_2, ("D", "o"): d_mlp_out,
                      ("D", "dn"): d_down_masked, ("D", "up"): d_final}
            run(dve, steps)


COLS = [("emb_g", 2), ("emb_b", 2)] + [(f"{n}{l}", 2) for l in range(2) for n in ("x1_g", "x1_b", "ln2_g", "ln2_b")] \
    + [("r_g", 2), ("r_b", 2), ("a_g", 2), ("a_b", 2), ("f_g", 2), ("f_b", 2)] \
    + [("r_in_b", 1), ("r_o1_b", 1), ("r_o2_b", 1)] + [(f"b1{l}", NFC) for l in range(2)] + [("fc1_b", NFC)]


def lay_out(np, a):
    f = np.float32

    def chunks(w, bias=None):
        n = w.shape[1]
        w = w.reshape(2, HC, n).transpose(1, 0, 2)
        if bias is not None:
            w = np.concatenate([w, np.stack([np.zeros(n, f), bias])[None]], 0)
        return np.ascontiguousarray(w)

    def deep(w):
        return np.ascontiguousarray(w.reshape(-1, P, w.shape[1]).transpose(1, 0, 2))

    def rows(v):
        return np.ascontiguousarray(np.broadcast_to(v, (P,) + v.shape))

    t, at, fn = (lambda n: a["L0_tok_" + n]), (lambda n: a["L0_attn_" + n]), (lambda n: a["L0_ffn_" + n])
    d = {"word_emb": t("word_emb"), "ident": np.eye(P, dtype=f)}
    d["shifts"] = np.stack([np.eye(P, k=-1, dtype=f), np.eye(P, dtype=f), np.eye(P, k=1, dtype=f)], 1)
    for l in range(2):
        d[f"tok_qkv{l}"] = chunks(np.concatenate([t("Wq")[l], t("Wk")[l], t("Wv")[l]], 1),
                                  np.concatenate([t("bq")[l], t("bk")[l], t("bv")[l]]))
        d[f"tok_o{l}"] = chunks(t("Wo")[l])
        d[f"tok_w1{l}"] = deep(np.concatenate([t("W1")[l], t("W1")[l, P:]]))
        d[f"tok_w2{l}"] = deep(t("W2")[l])
    d["tok_gate"] = chunks(t("Wg"), t("bg"))
    for name, n in (("gains", "g"), ("norm_shift", "b")):
        d[name] = rows(np.stack([t("emb_ln_" + n), t("ln1_" + n)[0], t("ln2_" + n)[0], t("ln1_" + n)[1],
                                 t("ln2_" + n)[1]]))
    d["out_bias"] = rows(np.stack([t("bo")[0], t("b2")[0], t("bo")[1], t("b2")[1]]))
    cols = np.zeros((P, 64), f)
    vectors = {"emb_g": t("emb_ln_g"), "emb_b": t("emb_ln_b"), "r_g": fn("r_ln_g"), "r_b": fn("r_ln_b"),
               "a_g": fn("ln1_g"), "a_b": fn("ln1_b"), "f_g": fn("ln2_g"), "f_b": fn("ln2_b"),
               "r_in_b": fn("r_in_b"), "r_o1_b": fn("r_o1_b"), "r_o2_b": fn("r_o2_b"), "fc1_b": fn("fc1_b")}
    for l in range(2):
        vectors |= {f"{n}{l}": t(n)[l] for n in ("ln2_g", "ln2_b", "b1")}
        vectors |= {f"x1_{n}{l}": np.concatenate([t(f"ln1_{n}")[l], t(f"ln1_{n}")[l, P:]]) for n in "gb"}
    c = 0
    for name, n in COLS:
        v = vectors[name].reshape(n, -1)
        cols[0:v.shape[1], c:c + n] = v.T
        c += n
    d["cols"] = cols
    d["pos3"] = rows(t("pos_emb3").reshape(-1))
    d["type0"] = rows(t("type_emb")[0])
    d["pos2"] = t("pos_emb2")
    d["type2"] = rows(t("type_emb2"))
    d["norm_gb"] = rows(np.stack([t("norm_g"), t("norm_b")]))
    d["proj_b"] = rows(at("proj_b"))
    d["fc2_b"] = rows(fn("fc2_b"))
    first = np.zeros((P, 2), f)
    first[0] = 1.0
    d["first"] = first
    d["att_qkv"] = chunks(np.ascontiguousarray(at("qkv_w").T), at("qkv_b"))
    d["att_proj"] = deep(np.ascontiguousarray(at("proj_w").T))

    def spread(w, b):
        ws, bs = np.zeros((H, 3, 4, 32), f), np.zeros((3, 4, 32), f)
        ws[..., 0:DH] = w.T.reshape(H, 3, 4, DH)
        bs[..., 0:DH] = b.reshape(3, 4, DH)
        return ws.reshape(H, 3 * P), bs.reshape(-1)

    (wq, bq), (wk, bk) = spread(fn("wq"), fn("bq")), spread(fn("wk"), fn("bk"))
    d["ffn_qk"] = chunks(np.concatenate([wq, wk], 1), np.concatenate([bq, bk]))
    d["ffn_v"] = chunks(np.ascontiguousarray(fn("wv").T), fn("bv"))
    d["ffn_o"] = chunks(np.ascontiguousarray(fn("wo").T), fn("bo"))
    d["ffn_fc1"] = chunks(np.ascontiguousarray(fn("fc1_w").T))
    d["ffn_fc2"] = deep(np.ascontiguousarray(fn("fc2_w").T))
    d["ffn_rin"] = chunks(np.ascontiguousarray(fn("r_in_w").T))
    d["ffn_ro1"] = deep(np.ascontiguousarray(fn("r_o1_w").T))
    d["ffn_ro2"] = np.ascontiguousarray(fn("r_o2_w").T)
    d["ffn_ro3"] = np.concatenate([fn("r_o3_w").T, fn("r_o3_b")[None]], 0)
    d["ffn_down"] = chunks(np.ascontiguousarray(fn("lra_down").reshape(NSLOT * RANK, H).T))
    d["ffn_up"] = chunks(np.ascontiguousarray(fn("lra_up").transpose(0, 2, 1).reshape(NSLOT * RANK, H)))
    x = a["x"]
    win = np.zeros((P, ROWS, NSLOT), x.dtype)
    win[1:, :, 0] = x.T[:-1]
    win[:, :, 1] = x.T
    win[:-1, :, 2] = x.T[1:]
    d["ids"] = win.reshape(P, ROWS * NSLOT)
    d["kinds"] = np.ascontiguousarray(a["mask_BS_i0_1"].T)
    return d


def kernel(**inputs):
    import numpy as np
    import concourse.bacc as bacc
    from concourse.bass_utils import run_bass_kernel_spmd

    nc = bacc.Bacc("TRN2", target_bir_lowering=False, num_devices=1)
    arrays = {f"in_{k}": np.ascontiguousarray(v) for k, v in lay_out(np, {k: np.asarray(v) for k, v in inputs.items()}).items()}
    d = {k[3:]: nc.dram_tensor(k, v.shape, mybir.dt.from_np(v.dtype), kind="ExternalInput").ap()
         for k, v in arrays.items()}
    out = nc.dram_tensor("out_dram", (ROWS * P, H), F32, kind="ExternalOutput").ap()
    build_tower(nc, d, out)
    r = run_bass_kernel_spmd(nc, [arrays], core_ids=[0])
    return r.results[0]["out_dram"].reshape(ROWS, P, H)
```
